# Optimizing a Trainium2 kernel written in Bass

```python
import numpy as np
import jax
import jax.numpy as jnp

def _softmax(x, axis=-1):
    return jax.nn.softmax(x, axis=axis)
def _gelu(x):
    return jax.nn.gelu(x, approximate=True)
def _silu(x):
    return jax.nn.silu(x)
def _sigmoid(x):
    return jax.nn.sigmoid(x)
def _layernorm(x, axis=-1, eps=1e-5):
    m = jnp.mean(x, axis=axis, keepdims=True)
    v = jnp.var(x, axis=axis, keepdims=True)
    return (x - m) / jnp.sqrt(v + eps)
def _scatter_add(tgt, idx, src, axis=0):
    return tgt.at[idx].add(src)
def _segment_sum(src, seg, n):
    return jax.ops.segment_sum(src, seg, n)

kernel_name = 'mk_conv_seq_d2_conv_nchw256_44b6dc'

def setup_inputs(seed: int = 0):
    np.random.seed(seed)
    _w = jnp.asarray
    def _rec_inputs():
        import jax
        import jax.numpy as jnp
        _gk = jax.random.key(seed)
        x = -0.0005153 + 1.001 * jax.random.normal(jax.random.fold_in(_gk, 1), (4, 256, 56, 56), jnp.float32)
        return x
    x = _rec_inputs()
    def _L0_conv_setup():
        import jax, jax.numpy as jnp
        import numpy as np
        BN_EPS = 1e-05

        def conv1x1(x, w, b):
            return jnp.einsum('bchw,oc->bohw', x, w) + b[None, :, None, None]
        key = jax.random.key(seed)
        ks = jax.random.split(key, 12)
        C, Ci = (256, 128)
        B, H, W = (4, 56, 56)
        s = 1.0 / np.sqrt(C)
        si = 1.0 / np.sqrt(Ci)
        return {'x': jax.random.normal(ks[0], (B, C, H, W), jnp.float32), 'w_theta': jax.random.normal(ks[1], (Ci, C), jnp.float32) * s, 'b_theta': jax.random.normal(ks[2], (Ci,), jnp.float32) * s, 'w_phi': jax.random.normal(ks[3], (Ci, C), jnp.float32) * s, 'b_phi': jax.random.normal(ks[4], (Ci,), jnp.float32) * s, 'w_g': jax.random.normal(ks[5], (Ci, C), jnp.float32) * s, 'b_g': jax.random.normal(ks[6], (Ci,), jnp.float32) * s, 'w_rec': jax.random.normal(ks[7], (C, Ci), jnp.float32) * si, 'b_rec': jax.random.normal(ks[8], (C,), jnp.float32) * si, 'bn_gamma': jax.random.normal(ks[9], (C,), jnp.float32) * 0.1 + 1.0, 'bn_beta': jax.random.normal(ks[10], (C,), jnp.float32) * 0.1, 'bn_mean': jax.random.normal(ks[11], (C,), jnp.float32) * 0.1, 'bn_var': jnp.ones((C,), jnp.float32)}
    _L0_conv_all = _L0_conv_setup()
    _L0_conv_in = {k: v for k, v in _L0_conv_all.items() if k in ('w_theta', 'b_theta', 'w_phi', 'b_phi', 'w_g', 'b_g', 'w_rec', 'b_rec', 'bn_gamma', 'bn_beta', 'bn_mean', 'bn_var', )}
    del _L0_conv_all

    def _L1_conv_setup():
        import jax, jax.numpy as jnp
        import numpy as np
        D_MODEL = 256
        D_INNER = 512
        D_STATE = 16
        DT_RANK = 16
        D_CONV = 4
        B, H, W = (2, 64, 64)

        def _mamba(u, in_w, conv_w, conv_b, xp_w, dt_w, dt_b, A_log, Dp, out_w):
            Bb, L, _ = u.shape
            xz = u @ in_w.T
            x, z = jnp.split(xz, 2, axis=-1)
            xpad = jnp.pad(x, ((0, 0), (D_CONV - 1, 0), (0, 0)))
            xc = conv_b + sum((xpad[:, k:k + L, :] * conv_w[:, k] for k in range(D_CONV)))
            x = jax.nn.silu(xc)
            xdbl = x @ xp_w.T
            dt = jax.nn.softplus(xdbl[..., :DT_RANK] @ dt_w.T + dt_b)
            Bm = xdbl[..., DT_RANK:DT_RANK + D_STATE]
            Cm = xdbl[..., DT_RANK + D_STATE:]
            A = -jnp.exp(A_log)
            dA = jnp.exp(dt[..., None] * A)
            dBx = (dt * x)[..., None] * Bm[:, :, None, :]

            def step(h, inp):
                a, bx, c = inp
                h = a * h + bx
                return (h, jnp.einsum('bdn,bn->bd', h, c))
            h0 = jnp.zeros((Bb, D_INNER, D_STATE), u.dtype)
            _, ys = jax.lax.scan(step, h0, (jnp.swapaxes(dA, 0, 1), jnp.swapaxes(dBx, 0, 1), jnp.swapaxes(Cm, 0, 1)))
            y = jnp.swapaxes(ys, 0, 1) + x * Dp
            y = y * jax.nn.silu(z)
            return y @ out_w.T
        key = jax.random.key(seed)
        ks = jax.random.split(key, 24)

        def rn(k, shape, s):
            return jax.random.normal(k, shape, jnp.float32) * s
        inp = {'x': rn(ks[0], (B, D_MODEL, H, W), 1.0)}
        for i, base in ((1, 1), (2, 10)):
            inp['in_proj_w%d' % i] = rn(ks[base + 0], (2 * D_INNER, D_MODEL), D_MODEL ** (-0.5))
            inp['conv_w%d' % i] = rn(ks[base + 1], (D_INNER, D_CONV), 0.3)
            inp['conv_b%d' % i] = jnp.zeros((D_INNER,), jnp.float32)
            inp['x_proj_w%d' % i] = rn(ks[base + 2], (DT_RANK + 2 * D_STATE, D_INNER), D_INNER ** (-0.5))
            inp['dt_proj_w%d' % i] = rn(ks[base + 3], (D_INNER, DT_RANK), DT_RANK ** (-0.5))
            dtv = jax.random.uniform(ks[base + 4], (D_INNER,), jnp.float32, 0.001, 0.1)
            inp['dt_proj_b%d' % i] = jnp.log(jnp.expm1(dtv))
            inp['A_log%d' % i] = jnp.log(jnp.tile(jnp.arange(1, D_STATE + 1, dtype=jnp.float32), (D_INNER, 1)))
            inp['D%d' % i] = jnp.ones((D_INNER,), jnp.float32)
            inp['out_proj_w%d' % i] = rn(ks[base + 5], (D_MODEL, D_INNER), D_INNER ** (-0.5))
        inp['cat_conv_w'] = rn(ks[22], (D_MODEL, 2 * D_MODEL), (2 * D_MODEL) ** (-0.5))
        inp['cat_conv_b'] = jnp.zeros((D_MODEL,), jnp.float32)
        return inp
    _L1_conv_all = _L1_conv_setup()
    _L1_conv_in = {k: v for k, v in _L1_conv_all.items() if k in ('in_proj_w1', 'conv_w1', 'conv_b1', 'x_proj_w1', 'dt_proj_w1', 'dt_proj_b1', 'A_log1', 'D1', 'out_proj_w1', 'in_proj_w2', 'conv_w2', 'conv_b2', 'x_proj_w2', 'dt_proj_w2', 'dt_proj_b2', 'A_log2', 'D2', 'out_proj_w2', 'cat_conv_w', 'cat_conv_b', )}
    del _L1_conv_all

    return {
        "x": x,
        "L0_conv_w_theta": _L0_conv_in["w_theta"],
        "L0_conv_b_theta": _L0_conv_in["b_theta"],
        "L0_conv_w_phi": _L0_conv_in["w_phi"],
        "L0_conv_b_phi": _L0_conv_in["b_phi"],
        "L0_conv_w_g": _L0_conv_in["w_g"],
        "L0_conv_b_g": _L0_conv_in["b_g"],
        "L0_conv_w_rec": _L0_conv_in["w_rec"],
        "L0_conv_b_rec": _L0_conv_in["b_rec"],
        "L0_conv_bn_gamma": _L0_conv_in["bn_gamma"],
        "L0_conv_bn_beta": _L0_conv_in["bn_beta"],
        "L0_conv_bn_mean": _L0_conv_in["bn_mean"],
        "L0_conv_bn_var": _L0_conv_in["bn_var"],
        "L1_conv_in_proj_w1": _L1_conv_in["in_proj_w1"],
        "L1_conv_conv_w1": _L1_conv_in["conv_w1"],
        "L1_conv_conv_b1": _L1_conv_in["conv_b1"],
        "L1_conv_x_proj_w1": _L1_conv_in["x_proj_w1"],
        "L1_conv_dt_proj_w1": _L1_conv_in["dt_proj_w1"],
        "L1_conv_dt_proj_b1": _L1_conv_in["dt_proj_b1"],
        "L1_conv_A_log1": _L1_conv_in["A_log1"],
        "L1_conv_D1": _L1_conv_in["D1"],
        "L1_conv_out_proj_w1": _L1_conv_in["out_proj_w1"],
        "L1_conv_in_proj_w2": _L1_conv_in["in_proj_w2"],
        "L1_conv_conv_w2": _L1_conv_in["conv_w2"],
        "L1_conv_conv_b2": _L1_conv_in["conv_b2"],
        "L1_conv_x_proj_w2": _L1_conv_in["x_proj_w2"],
        "L1_conv_dt_proj_w2": _L1_conv_in["dt_proj_w2"],
        "L1_conv_dt_proj_b2": _L1_conv_in["dt_proj_b2"],
        "L1_conv_A_log2": _L1_conv_in["A_log2"],
        "L1_conv_D2": _L1_conv_in["D2"],
        "L1_conv_out_proj_w2": _L1_conv_in["out_proj_w2"],
        "L1_conv_cat_conv_w": _L1_conv_in["cat_conv_w"],
        "L1_conv_cat_conv_b": _L1_conv_in["cat_conv_b"],
    }

def reference(x, L0_conv_w_theta, L0_conv_b_theta, L0_conv_w_phi, L0_conv_b_phi, L0_conv_w_g, L0_conv_b_g, L0_conv_w_rec, L0_conv_b_rec, L0_conv_bn_gamma, L0_conv_bn_beta, L0_conv_bn_mean, L0_conv_bn_var, L1_conv_in_proj_w1, L1_conv_conv_w1, L1_conv_conv_b1, L1_conv_x_proj_w1, L1_conv_dt_proj_w1, L1_conv_dt_proj_b1, L1_conv_A_log1, L1_conv_D1, L1_conv_out_proj_w1, L1_conv_in_proj_w2, L1_conv_conv_w2, L1_conv_conv_b2, L1_conv_x_proj_w2, L1_conv_dt_proj_w2, L1_conv_dt_proj_b2, L1_conv_A_log2, L1_conv_D2, L1_conv_out_proj_w2, L1_conv_cat_conv_w, L1_conv_cat_conv_b):
    import jax
    import jax.numpy as jnp
    def _L0_conv_ref(x, w_theta, b_theta, w_phi, b_phi, w_g, b_g, w_rec, b_rec, bn_gamma, bn_beta, bn_mean, bn_var):
        import jax, jax.numpy as jnp
        import numpy as np
        BN_EPS = 1e-05

        def conv1x1(x, w, b):
            return jnp.einsum('bchw,oc->bohw', x, w) + b[None, :, None, None]
        b, _, h, w = x.shape
        n = h * w
        c = w_theta.shape[0]
        theta_x = conv1x1(x, w_theta, b_theta).reshape(b, c, n).transpose(0, 2, 1)
        phi_x = conv1x1(x, w_phi, b_phi).reshape(b, c, n)
        g_x = conv1x1(x, w_g, b_g).reshape(b, c, n).transpose(0, 2, 1)
        attention = jnp.matmul(theta_x, phi_x) / n
        out = jnp.matmul(attention, g_x).transpose(0, 2, 1).reshape(b, c, h, w)
        out = conv1x1(out, w_rec, b_rec)
        inv = bn_gamma / jnp.sqrt(bn_var + BN_EPS)
        out = out * inv[None, :, None, None] + (bn_beta - bn_mean * inv)[None, :, None, None]
        return out + x

    def _L1_conv_ref(x, in_proj_w1, conv_w1, conv_b1, x_proj_w1, dt_proj_w1, dt_proj_b1, A_log1, D1, out_proj_w1, in_proj_w2, conv_w2, conv_b2, x_proj_w2, dt_proj_w2, dt_proj_b2, A_log2, D2, out_proj_w2, cat_conv_w, cat_conv_b):
        import jax, jax.numpy as jnp
        import numpy as np
        D_MODEL = 256
        D_INNER = 512
        D_STATE = 16
        DT_RANK = 16
        D_CONV = 4
        B, H, W = (2, 64, 64)

        def _mamba(u, in_w, conv_w, conv_b, xp_w, dt_w, dt_b, A_log, Dp, out_w):
            Bb, L, _ = u.shape
            xz = u @ in_w.T
            x, z = jnp.split(xz, 2, axis=-1)
            xpad = jnp.pad(x, ((0, 0), (D_CONV - 1, 0), (0, 0)))
            xc = conv_b + sum((xpad[:, k:k + L, :] * conv_w[:, k] for k in range(D_CONV)))
            x = jax.nn.silu(xc)
            xdbl = x @ xp_w.T
            dt = jax.nn.softplus(xdbl[..., :DT_RANK] @ dt_w.T + dt_b)
            Bm = xdbl[..., DT_RANK:DT_RANK + D_STATE]
            Cm = xdbl[..., DT_RANK + D_STATE:]
            A = -jnp.exp(A_log)
            dA = jnp.exp(dt[..., None] * A)
            dBx = (dt * x)[..., None] * Bm[:, :, None, :]

            def step(h, inp):
                a, bx, c = inp
                h = a * h + bx
                return (h, jnp.einsum('bdn,bn->bd', h, c))
            h0 = jnp.zeros((Bb, D_INNER, D_STATE), u.dtype)
            _, ys = jax.lax.scan(step, h0, (jnp.swapaxes(dA, 0, 1), jnp.swapaxes(dBx, 0, 1), jnp.swapaxes(Cm, 0, 1)))
            y = jnp.swapaxes(ys, 0, 1) + x * Dp
            y = y * jax.nn.silu(z)
            return y @ out_w.T
        b, c, h, w = x.shape
        x1 = x.reshape(b * h, w, c)
        x2 = x.reshape(b * w, h, c)
        y1 = _mamba(x1, in_proj_w1, conv_w1, conv_b1, x_proj_w1, dt_proj_w1, dt_proj_b1, A_log1, D1, out_proj_w1).reshape(b, c, h, w)
        y2 = _mamba(x2, in_proj_w2, conv_w2, conv_b2, x_proj_w2, dt_proj_w2, dt_proj_b2, A_log2, D2, out_proj_w2).reshape(b, c, h, w)
        cat = jnp.concatenate([y1, y2], axis=1)
        out = jnp.einsum('oc,bchw->bohw', cat_conv_w, cat) + cat_conv_b[None, :, None, None]
        return out + x

    def _gn(v, G=32, eps=1e-5):
        B_, C_, H_, W_ = v.shape
        g = v.reshape(B_, G, C_ // G, H_, W_)
        m = jnp.mean(g, axis=(2, 3, 4), keepdims=True)
        s = jnp.var(g, axis=(2, 3, 4), keepdims=True)
        return ((g - m) / jnp.sqrt(s + eps)).reshape(v.shape)

    def _ln_c(v, eps=1e-6):
        m = jnp.mean(v, axis=1, keepdims=True)
        s = jnp.var(v, axis=1, keepdims=True)
        return (v - m) / jnp.sqrt(s + eps)

    def _ln_t(v, eps=1e-5):
        m = jnp.mean(v, axis=-1, keepdims=True)
        s = jnp.var(v, axis=-1, keepdims=True)
        return (v - m) / jnp.sqrt(s + eps)

    def _to_tokens(v):
        B_, C_, H_, W_ = v.shape
        return v.reshape(B_, C_, H_ * W_).transpose(0, 2, 1)
    def _from_tokens(t, like):
        B_, C_, H_, W_ = like.shape
        return t.transpose(0, 2, 1).reshape(B_, C_, H_, W_)

    x = _L0_conv_ref(x, L0_conv_w_theta, L0_conv_b_theta, L0_conv_w_phi, L0_conv_b_phi, L0_conv_w_g, L0_conv_b_g, L0_conv_w_rec, L0_conv_b_rec, L0_conv_bn_gamma, L0_conv_bn_beta, L0_conv_bn_mean, L0_conv_bn_var)
    x = _L1_conv_ref(x, L1_conv_in_proj_w1, L1_conv_conv_w1, L1_conv_conv_b1, L1_conv_x_proj_w1, L1_conv_dt_proj_w1, L1_conv_dt_proj_b1, L1_conv_A_log1, L1_conv_D1, L1_conv_out_proj_w1, L1_conv_in_proj_w2, L1_conv_conv_w2, L1_conv_conv_b2, L1_conv_x_proj_w2, L1_conv_dt_proj_w2, L1_conv_dt_proj_b2, L1_conv_A_log2, L1_conv_D2, L1_conv_out_proj_w2, L1_conv_cat_conv_w, L1_conv_cat_conv_b)
    return x


_drawn_inputs = setup_inputs


def setup_inputs(seed=0):
    import zlib

    import numpy as np

    out = dict(_drawn_inputs(seed))
    spreads = {'L0_conv_bn_var': (1.0, 0.2),
     'L1_conv_conv_b1': (0.0, 0.28),
     'L1_conv_D1': (1.0, 0.6),
     'L1_conv_conv_b2': (0.0, 0.307),
     'L1_conv_D2': (1.0, 0.6),
     'L1_conv_cat_conv_b': (0.0, 0.8)}
    factors = {'L1_conv_x_proj_w1': 3.185,
     'L1_conv_dt_proj_w1': 6.416,
     'L1_conv_dt_proj_b1': 7.429,
     'L1_conv_A_log1': 7.151,
     'L1_conv_x_proj_w2': 4.027,
     'L1_conv_dt_proj_w2': 8.0,
     'L1_conv_dt_proj_b2': 8.0,
     'L1_conv_A_log2': 8.0}
    for name, (base, spread) in spreads.items():
        noise = np.random.default_rng([zlib.crc32(name.encode()), seed]).standard_normal(out[name].shape)
        drawn = base * np.exp(spread * noise) if base else spread * noise
        out[name] = jnp.asarray(drawn.astype(out[name].dtype))
    for name, factor in factors.items():
        out[name] = (out[name] * factor).astype(out[name].dtype)
    return out
```

```python
from contextlib import ExitStack

import concourse.bass as bass
from concourse import mybir

BATCH, CH, SIDE = 4, 256, 56
NPOS = SIDE * SIDE
CMID = 128
DIN, NST, DTR, DCONV = 512, 16, 16, 4
SEQ, FEAT = SIDE, CH
TSEQ = 8
T = TSEQ * SEQ
TPB = NPOS // T
TILES = BATCH * TPB
DB = DIN // 128
GP = NST // 2
SLOTS = DB * GP
XPM = 3 * 2 * NST + DTR
TCH = T // 4
HALF = NPOS // 28
NBLK = NPOS // 64

W_IN, W_OUT, W_XP = 0, 2 * 2 * DIN, 2 * 2 * DIN + DB * FEAT
W_DT = W_XP + DB * XPM
W_CW = W_DT + DIN
W_CB = W_CW + DB * DCONV
W_D = W_CB + DB
W_A = W_D + DB
W_COLS = W_A + DB * NST
KCOLS = 2 * CH + 2

BN_EPS = 1e-5
RESTART, A_TOP = 1e28, -1e-25

fp32, bf16 = mybir.dt.float32, mybir.dt.bfloat16
ALU, ACT = mybir.AluOpType, mybir.ActivationFunctionType
EXP_SET = "exp_and_others"

ITEMS = 4 + 2 + 2 * DB + 1 + DB + 4 * (GP - 1)
FRONT_ITEMS = ITEMS - 6

RING = 4
BX0, HC0, SD0, GR0, YG0, ST0 = SLOTS, SLOTS, RING, 2, 2 * DB, 16


def view(t, offset, dims, parts=128, first=0):
    row = t.shape[1]
    return bass.AP(tensor=t, offset=first * row + offset, ap=[[row, parts]] + [list(d) for d in dims])


def prepare(nc, a, w_dram, cat_dram, keep):
    with ExitStack() as ctx:
        sb = lambda name, cols, parts=128: ctx.enter_context(nc.sbuf_tensor(name, [parts, cols], fp32))
        sem = lambda name: ctx.enter_context(nc.semaphore(name))
        ps = ctx.enter_context(nc.psum_tensor("prep_ps", [128, 8 * 512], fp32))
        raw_in = [sb(f"raw_in{m}", 8 * 256) for m in range(2)]
        raw_out = [sb(f"raw_out{m}", 2 * 512) for m in range(2)]
        raw_xp = [sb(f"raw_xp{m}", 512) for m in range(2)]
        raw_dt = [sb(f"raw_dt{m}", DB * DTR) for m in range(2)]
        raw_a = [sb(f"raw_a{m}", DB * NST) for m in range(2)]
        pack = [sb(f"pack{m}", W_COLS) for m in range(2)]
        raw_cat, raw_pg, raw_rec = sb("raw_cat", 2 * 512), sb("raw_pg", 2 * 256), sb("raw_rec", 2 * 128)
        cat_t = sb("cat_t", 4 * 256)
        W2 = CH + 2
        bn = sb("bn", 5 * W2)
        root = sb("root", 2 * W2)
        ident, wpg, wrec, invn, cst = keep["ident"], keep["wpg"], keep["wrec"], keep["invn"], keep["cst"]
        loaded, cleared, placed = sem("prep_loaded"), sem("prep_cleared"), sem("prep_placed")
        turned, copied = sem("prep_turned"), sem("prep_copied")
        a_exp, bn_root, chain, stored = sem("prep_a_exp"), sem("prep_root"), sem("prep_chain"), sem("prep_stored")

        jobs = []
        for m in range(2):
            for k in range(2):
                for h in range(2):
                    src = [raw_in[m][:, (4 * h + r) * 256 + k * 128:(4 * h + r) * 256 + (k + 1) * 128] for r in range(4)]
                    o = W_IN + k * 2 * DIN + h * 512
                    jobs.append((src, 128, 128, pack[m][:, o:o + 512]))
            for jj in range(2):
                src = [raw_out[m][:, fc * 512 + j * 128:fc * 512 + (j + 1) * 128] for j in (2 * jj, 2 * jj + 1) for fc in range(2)]
                jobs.append((src, 128, 128, pack[m][:, W_OUT + jj * 512:W_OUT + (jj + 1) * 512]))
            src = [raw_xp[m][0:XPM, j * 128:(j + 1) * 128] for j in range(DB)]
            jobs.append((src, 128, XPM, pack[m][:, W_XP:W_XP + DB * XPM]))
            src = [raw_dt[m][:, j * DTR:(j + 1) * DTR] for j in range(DB)]
            jobs.append((src, DTR, 128, pack[m][0:DTR, W_DT:W_DT + DIN]))
        for jj in range(2):
            src = [raw_cat[:, oc * 512 + j * 128:oc * 512 + (j + 1) * 128] for j in (2 * jj, 2 * jj + 1) for oc in range(2)]
            jobs.append((src, 128, 128, cat_t[:, jj * 512:(jj + 1) * 512]))
        src = [raw_pg[:, w * 256 + k * 128:w * 256 + (k + 1) * 128] for k in range(2) for w in range(2)]
        jobs.append((src, 128, 128, wpg[:, :]))
        jobs.append(([raw_rec[:, oc * 128:(oc + 1) * 128] for oc in range(2)], 128, 128, wrec[:, :]))

        loads = [(ident[:, :], a["ident"]), (keep["sel"][:, :], a["sel"])]
        for m in range(2):
            n = str(m + 1)
            loads.append((raw_in[m][:, :].rearrange("p (r c) -> p r c", r=8), a["L1_conv_in_proj_w" + n].rearrange("(r p) c -> p r c", p=128)))
            loads.append((raw_out[m][:, :].rearrange("p (r c) -> p r c", r=2), a["L1_conv_out_proj_w" + n].rearrange("(r p) c -> p r c", p=128)))
            xp = a["L1_conv_x_proj_w" + n]
            for r in range(3):
                loads.append((raw_xp[m][32 * r:32 * r + 32, :], xp[DTR:DTR + 2 * NST, :]))
            loads.append((raw_xp[m][96:96 + DTR, :], xp[0:DTR, :]))
            loads.append((raw_dt[m][:, :].rearrange("p (j c) -> p j c", j=DB), a["L1_conv_dt_proj_w" + n].rearrange("(j p) c -> p j c", p=128)))
            loads.append((raw_a[m][:, :].rearrange("p (j c) -> p j c", j=DB), a["L1_conv_A_log" + n].rearrange("(j p) c -> p j c", p=128)))
        loads.append((raw_cat[:, :].rearrange("p (r c) -> p r c", r=2), a["L1_conv_cat_conv_w"].rearrange("(r p) c -> p r c", p=128)))
        loads.append((raw_pg[:, 0:256], a["L0_conv_w_phi"]))
        loads.append((raw_pg[:, 256:512], a["L0_conv_w_g"]))
        loads.append((raw_rec[:, :].rearrange("p (r c) -> p r c", r=2), a["L0_conv_w_rec"].rearrange("(r p) c -> p r c", p=128)))
        loads.append((keep["wtheta"][:, :], a["L0_conv_w_theta"]))
        loads.append((keep["btheta"][:, :], a["L0_conv_b_theta"].unsqueeze(1)))
        loads.append((keep["pgbias"][:, 0:128], a["L0_conv_b_phi"].partition_broadcast(128)))
        loads.append((keep["pgbias"][:, 128:256], a["L0_conv_b_g"].partition_broadcast(128)))
        loads.append((keep["catb"][:, :], a["L1_conv_cat_conv_b"].rearrange("(o p) -> p o", p=128)))
        for i, n in enumerate(("bn_gamma", "bn_var", "bn_beta", "bn_mean", "b_rec")):
            loads.append((bn[:, i * W2:i * W2 + CH], a["L0_conv_" + n].partition_broadcast(128)))
            loads.append((bn[:, i * W2 + CH:(i + 1) * W2], a["L0_conv_" + n].rearrange("(o p) -> p o", p=128)))
        direct = []
        for m in range(2):
            n = str(m + 1)
            direct.append((pack[m][:, W_CW:W_CW + DB * DCONV].rearrange("p (j c) -> p j c", j=DB), a["L1_conv_conv_w" + n].rearrange("(j p) c -> p j c", p=128)))
            direct.append((pack[m][:, W_CB:W_CB + DB], a["L1_conv_conv_b" + n].rearrange("(j p) -> p j", p=128)))
            direct.append((pack[m][:, W_D:W_D + DB], a["L1_conv_D" + n].rearrange("(j p) -> p j", p=128)))
            direct.append((pack[m][DTR:DTR + 1, W_DT:W_DT + DIN], a["L1_conv_dt_proj_b" + n].unsqueeze(0)))

        with nc.Block() as block, nc.allow_non_contiguous_dma(reason="small per-channel vectors"):
            @block.sync
            def _(sp):
                for dst, src in loads:
                    sp.dma_start(dst, src).then_inc(loaded, 16)
                sp.wait_ge(cleared, 1)
                for dst, src in direct:
                    sp.dma_start(dst, src).then_inc(placed, 16)
                sp.wait_ge(placed, 16 * len(direct))
                sp.wait_ge(copied, len(jobs) + 2)
                for m in range(2):
                    sp.dma_start(w_dram[m], pack[m][:, :]).then_inc(stored, 16)
                sp.dma_start(cat_dram, cat_t[:, :]).then_inc(stored, 16)
                sp.wait_ge(stored, 48)

            @block.scalar
            def _(act):
                act.wait_ge(loaded, 16 * len(loads))
                act.wait_ge(chain, 1)
                nc.scalar.activation(root[:, 0:W2], bn[:, W2:2 * W2], ACT.Sqrt).then_inc(bn_root, 1)
                for m in range(2):
                    nc.scalar.activation(raw_a[m][:, :], raw_a[m][:, :], ACT.Exp).then_inc(a_exp, 1)

            @block.tensor
            def _(pe):
                pe.wait_ge(loaded, 16 * len(loads))
                for i, (srcs, rows, cols, _) in enumerate(jobs):
                    if i >= 4:
                        pe.wait_ge(copied, i - 3)
                    for r, s in enumerate(srcs):
                        o = (i % 4) * 512 + r * cols
                        p = s.shape[0]
                        last = nc.tensor.transpose(ps[0:rows, o:o + cols], s, ident[0:p, 0:p])
                    last.then_inc(turned, 1)

            @block.vector
            def _(dve):
                for m in range(2):
                    last = nc.vector.memset(pack[m][:, W_DT:W_DT + DIN], 0.0)
                last.then_inc(cleared, 1)
                dve.wait_ge(loaded, 16 * len(loads))
                gamma, var, beta, mean, brec = (bn[:, i * W2:(i + 1) * W2] for i in range(5))
                nc.vector.tensor_scalar_add(var, var, BN_EPS).then_inc(chain, 1)
                dve.wait_ge(cleared, 1)
                for i, (srcs, rows, cols, dst) in enumerate(jobs):
                    dve.wait_ge(turned, i + 1)
                    o = (i % 4) * 512
                    nc.vector.tensor_copy(dst, ps[0:rows, o:o + len(srcs) * cols]).then_inc(copied, 1)
                for m in range(2):
                    dve.wait_ge(a_exp, m + 1)
                    nc.vector.tensor_scalar(pack[m][:, W_A:W_A + DB * NST], raw_a[m][:, :], -1.0, A_TOP, ALU.mult, ALU.min).then_inc(copied, 1)
                count = [1]

                def link(ins):
                    count[0] += 1
                    ins.then_inc(chain, 1)
                    dve.wait_ge(chain, count[0])

                r, s = root[:, 0:W2], root[:, W2:2 * W2]
                dve.wait_ge(bn_root, 1)
                link(nc.vector.reciprocal(r, r))
                link(nc.vector.tensor_tensor(s, r, r, ALU.mult))
                link(nc.vector.tensor_tensor(s, s, var, ALU.mult))
                link(nc.vector.tensor_scalar(s, s, -0.5, 1.5, ALU.mult, ALU.add))
                link(nc.vector.tensor_tensor(r, r, s, ALU.mult))
                link(nc.vector.tensor_tensor(r, r, gamma, ALU.mult))
                link(nc.vector.tensor_tensor(s, brec, mean, ALU.subtract))
                link(nc.vector.tensor_tensor(s, s, r, ALU.mult))
                link(nc.vector.tensor_tensor(cst[:, :], s, beta, ALU.add))
                link(nc.vector.tensor_scalar_mul(invn[:, :], r, 1.0 / NPOS))
                link(nc.vector.tensor_tensor(keep["catb"][:, :], keep["catb"][:, :], cst[:, CH:CH + 2], ALU.add))
                link(nc.vector.memset(keep["id2"][:, :], 0.0))
                for k in range(2):
                    link(nc.vector.tensor_copy(keep["id2"][:, k * CH + k * 128:k * CH + (k + 1) * 128], ident[:, :]))
                nc.vector.tensor_copy(keep["btrep"][:, :], keep["btheta"][:, :].to_broadcast([128, 128])).then_inc(chain, 1)


def attention(nc, x_in, u_dram, k_dram, keep):
    PAIRS = 14
    UT = 13
    with ExitStack() as ctx:
        sb = lambda name, cols, parts=128: ctx.enter_context(nc.sbuf_tensor(name, [parts, cols], fp32))
        sem = lambda name: ctx.enter_context(nc.semaphore(name))
        ps = ctx.enter_context(nc.psum_tensor("att_ps", [128, 8 * 512], fp32))
        bank = lambda i: ps[:, i * 512:(i + 1) * 512]
        xb = [sb(f"xb{o}", 2 * NPOS) for o in range(2)]
        ub = [sb(f"ub{o}", 2 * NPOS) for o in range(2)]
        pg = [sb(f"pg{i}", 512) for i in range(2)]
        mt_sb, r_sb = sb("mt_sb", 128), sb("r_sb", CH)
        kn, kp, kb = sb("kn", KCOLS), sb("kp", 2 * CH), sb("kb", CH)
        x_ready = [sem(f"x_ready{o}") for o in range(2)]
        pg_ready, pg_taken, mt_step = sem("pg_ready"), sem("pg_taken"), sem("mt_step")
        k_pe, k_dve, k_stored = sem("k_pe"), sem("k_dve"), sem("k_stored")
        ut_ready, ut_taken = sem("ut_ready"), sem("ut_taken")
        u_stored = [sem(f"u_stored{o}") for o in range(2)]
        wpg, wrec, wtheta = keep["wpg"], keep["wrec"], keep["wtheta"]

        def group(cls, n):
            ks = [cls + 16 * n + 4 * i for i in range(4)]
            return [k for k in ks if k + 1 < NBLK]

        ut_items = [(cls, group(cls, n)) for n in range(3) for cls in (0, 2, 1, 3)] + [("edge", [])]
        assert len(ut_items) == UT

        def token_view(o, k, r, count, parts, first):
            at = []
            for rr in (r, r + 2):
                q = (rr + k) % 4
                if first:
                    q -= 1
                    at.append((q // 2) * NPOS + (NBLK * rr + k - q - 1) // 4)
                else:
                    at.append((q // 2) * NPOS + (NBLK * rr + k - q) // 4)
            return view(ub[o], at[0], [[1, count], [at[1] - at[0], 2], [NBLK, 64]], parts, first)

        with nc.Block() as block:
            @block.sync
            def _(sp):
                sp.sem_inc(ut_ready, 2 * UT)
                with sp.Fori(0, 2) as it:
                    for o in range(2):
                        b = sp.snap(it * 2 + o)
                        sp.wait_ge(ut_ready, it * (2 * UT) + (UT * (o - 1) + 2 * UT))
                        sp.dma_start(xb[o][:, :].rearrange("p (k n) -> p k n", k=2),
                                     x_in[bass.ds(b, 1)].rearrange("b (k p) n -> p (b k) n", p=128)).then_inc(x_ready[o], 16)

            @block.scalar
            def _(act):
                for o in range(2):
                    act.sem_inc(u_stored[o], 16)
                with act.Fori(0, 2) as it:
                    for o in range(2):
                        act.wait_ge(k_dve, it * 8 + (4 * o + 3))
                        act.dma_start(k_dram[bass.ds(it * 2 + o, 1)].rearrange("b p n -> p (b n)"), kn[:, :]).then_inc(k_stored, 16)
                        act.wait_ge(ut_taken, it * (2 * UT) + (UT * (o + 1) + 2))
                        for i in range(TPB):
                            act.dma_start(u_dram[bass.ds((it * 2 + o) * TPB + i, 1)].rearrange("t p (k n) -> p (t k) n", k=2),
                                          ub[o][:, :].rearrange("p (k n) -> p k n", k=2)[:, :, i * T:(i + 1) * T]).then_inc(u_stored[o], 16)
                act.wait_ge(k_stored, 16 * BATCH)
                for o in range(2):
                    act.wait_ge(u_stored[o], 16 + 2 * 16 * TPB)

            @block.tensor
            def _(pe):
                pe.sem_inc(pg_taken, 2)
                pe.sem_inc(ut_taken, 2)
                with pe.Fori(0, 2) as it:
                    for o in range(2):
                        P = lambda c: it * (2 * PAIRS) + (PAIRS * o + c)
                        U = lambda c: it * (2 * UT) + (UT * o + c)

                        def add_pair(i):
                            pe.wait_ge(pg_taken, P(i + 3))
                            for h in range(2):
                                s = pg[i % 2]
                                last = nc.tensor.matmul(bank(2)[:, 0:CMID], s[0:HALF, h * 256 + 128:h * 256 + 256],
                                                        s[0:HALF, h * 256:h * 256 + 128],
                                                        start=(i == 0 and h == 0), stop=(i == PAIRS - 1 and h == 1))
                            last.then_inc(mt_step, 1)

                        pe.wait_ge(x_ready[o], it * 16 + 16)
                        for i in range(PAIRS):
                            pe.wait_ge(pg_taken, P(i + 1))
                            for h in range(2):
                                n0 = (2 * i + h) * HALF
                                for k in range(2):
                                    last = nc.tensor.matmul(bank(i % 2)[0:HALF, h * 256:(h + 1) * 256],
                                                            xb[o][:, k * NPOS + n0:k * NPOS + n0 + HALF],
                                                            wpg[:, k * 256:(k + 1) * 256], start=(k == 0), stop=(k == 1))
                            last.then_inc(pg_ready, 1)
                            if i:
                                add_pair(i - 1)
                        add_pair(PAIRS - 1)
                        pe.wait_ge(k_dve, it * 8 + (4 * o + 1))
                        nc.tensor.matmul(bank(3)[:, 0:CH], mt_sb[:, :], wrec[:, :], start=True, stop=True).then_inc(k_pe, 1)
                        pe.wait_ge(k_dve, it * 8 + (4 * o + 2))
                        for k in range(2):
                            nc.tensor.matmul(bank(4)[:, k * CH:(k + 1) * CH], wtheta[:, k * 128:(k + 1) * 128], r_sb[:, :],
                                             start=True, stop=True)
                        nc.tensor.matmul(bank(5)[:, 0:CH], keep["btrep"][:, :], r_sb[:, :], start=True, stop=True)
                        for k in range(2):
                            last = nc.tensor.matmul(bank(5)[:, CH + k:CH + k + 1], r_sb[:, k * 128:(k + 1) * 128],
                                                    keep["btheta"][:, :], start=True, stop=True)
                        last.then_inc(k_pe, 1)
                        pe.wait_ge(k_dve, it * 8 + (4 * o + 4))
                        for i, (cls, ks) in enumerate(ut_items):
                            pe.wait_ge(ut_taken, U(i + 1))
                            b = bank(6 + (i + o) % 2)
                            if cls == "edge":
                                for rows, n0, par in ((0, 64 * (NBLK - 1), 0), (64, 0, 1)):
                                    for k2 in range(2):
                                        last = nc.tensor.matmul(b[rows:rows + 64, rows * 2:rows * 2 + 128],
                                                                xb[o][:, k2 * NPOS + n0:k2 * NPOS + n0 + 64],
                                                                kp[:, k2 * CH + par * 128:k2 * CH + par * 128 + 128],
                                                                start=(k2 == 0), stop=(k2 == 1))
                            for j, kk in enumerate(ks):
                                par = kk % 2
                                for k2 in range(2):
                                    n0 = k2 * NPOS + 64 * kk
                                    last = nc.tensor.matmul(b[:, j * 128:(j + 1) * 128], xb[o][:, n0:n0 + 128],
                                                            kp[:, k2 * CH + par * 128:k2 * CH + par * 128 + 128],
                                                            start=(k2 == 0), stop=(k2 == 1))
                            last.then_inc(ut_ready, 1)

            @block.vector
            def _(dve):
                dve.sem_inc(mt_step, 2)
                with dve.Fori(0, 2) as it:
                    for o in range(2):
                        P = lambda c: it * (2 * PAIRS) + (PAIRS * o + c)
                        K = lambda c: it * 8 + (4 * o + c)
                        for i in range(PAIRS):
                            dve.wait_ge(pg_ready, P(i + 1))
                            dve.wait_ge(mt_step, P(i + 1))
                            nc.vector.tensor_tensor(view(pg[i % 2], 0, [[256, 2], [1, 256]], HALF),
                                                    bank(i % 2)[0:HALF, :].rearrange("p (h c) -> p h c", h=2),
                                                    view(keep["pgbias"], 0, [[0, 2], [1, 256]], HALF), ALU.add).then_inc(pg_taken, 1)
                        dve.wait_ge(mt_step, P(PAIRS + 2))
                        nc.vector.tensor_copy(mt_sb[:, :], bank(2)[:, 0:CMID]).then_inc(k_dve, 1)
                        dve.wait_ge(k_pe, it * 4 + (2 * o + 1))
                        nc.vector.tensor_tensor(r_sb[:, :], bank(3)[:, 0:CH], keep["invn"][:, 0:CH], ALU.mult).then_inc(k_dve, 1)
                        dve.wait_ge(k_pe, it * 4 + (2 * o + 2))
                        if o == 0:
                            dve.wait_ge(keep["kn_free"], it * 1 + 1)
                        else:
                            dve.wait_ge(k_stored, it * 32 + 16)
                        nc.vector.tensor_tensor(kn[:, 0:2 * CH], bank(4), keep["id2"][:, :], ALU.add)
                        order = [[64, 2], [128, 2], [1, 64]]
                        nc.vector.tensor_tensor(view(kb, 0, order), view(ps, 5 * 512, [[2, 2], [1, 2], [4, 64]]),
                                                view(keep["cst"], 0, [[2, 2], [1, 2], [4, 64]]), ALU.add)
                        nc.vector.tensor_tensor(kn[:, 2 * CH:2 * CH + 2], bank(5)[:, CH:CH + 2], keep["catb"][:, :], ALU.add).then_inc(k_dve, 1)
                        dve.wait_ge(k_dve, K(3))
                        for k in range(2):
                            last = nc.vector.tensor_copy(view(kp, k * CH, order), view(kn, k * CH, [[2, 2], [1, 2], [4, 64]]))
                        last.then_inc(k_dve, 1)
                        dve.wait_ge(u_stored[o], it * (16 * TPB) + 16)
                        for i, (cls, ks) in enumerate(ut_items):
                            dve.wait_ge(ut_ready, it * (2 * UT) + (UT * o + i + 1 + 2 * UT))
                            if i == 0:
                                dve.wait_ge(k_dve, K(4))
                            b = (6 + (i + o) % 2) * 512
                            if cls == "edge":
                                nc.vector.tensor_tensor(token_view(o, NBLK - 1, 0, 1, 64, 0), view(ps, b, [[128, 1], [64, 2], [1, 64]], 64),
                                                        view(kb, 0, [[0, 1], [64, 2], [1, 64]], 64), ALU.add)
                                nc.vector.tensor_tensor(token_view(o, 0, 1, 1, 64, 64), view(ps, b + 128, [[128, 1], [64, 2], [1, 64]], 64, 64),
                                                        view(kb, 128, [[0, 1], [64, 2], [1, 64]], 64, 64), ALU.add).then_inc(ut_taken, 1)
                            else:
                                par = cls % 2
                                nc.vector.tensor_tensor(token_view(o, ks[0], par, len(ks), 128, 0),
                                                        view(ps, b, [[128, len(ks)], [64, 2], [1, 64]]),
                                                        view(kb, par * 128, [[0, len(ks)], [64, 2], [1, 64]]), ALU.add).then_inc(ut_taken, 1)

            @block.gpsimd
            def _(pool):
                pool.sem_inc(keep["kn_free"], 1)
                pool.wait_ge(k_stored, 32)
                pool.sem_inc(keep["kn_free"], 1)


def mambas(nc, u_dram, w_dram, y_dram, keep):
    with ExitStack() as ctx:
        sb = lambda name, cols, parts=128, dt=fp32: ctx.enter_context(nc.sbuf_tensor(name, [parts, cols], dt))
        sem = lambda name: ctx.enter_context(nc.semaphore(name))
        ps = ctx.enter_context(nc.psum_tensor("mamba_ps", [128, 8 * 512], fp32))
        bank = lambda i: ps[:, i * 512:(i + 1) * 512]
        decay = [ps[:, i * 1024:i * 1024 + 2 * T] for i in range(2)]
        y_ps = [bank(4)[:, 0:T], bank(5)[:, 0:T]]
        work = [bank(6), bank(7)]

        w = sb("w", W_COLS)
        u = [sb(f"u{p}", 2 * T) for p in range(2)]
        x = [sb(f"x{p}", DB * T) for p in range(2)]
        sz = [sb(f"sz{p}", DB * T) for p in range(2)]
        dt = [sb(f"dt{p}", DB * T) for p in range(2)]
        dtx = [sb(f"dtx{p}", DB * T) for p in range(2)]
        b_all, c_all = sb("b_all", NST * T), sb("c_all", NST * T)
        dbx = [sb(f"dbx{i}", 2 * T) for i in range(RING)]
        hc = [sb(f"hc{i}", 2 * T) for i in range(RING)]
        gx = [sb(f"gx{i}", T) for i in range(2)]
        yg = sb("yg", DB * T)
        ytok = sb("ytok", 4 * FEAT, TCH)
        parts, mid = sb("parts", T, 96, bf16), sb("mid", T, 96, bf16)
        rest = sb("rest", T, 96)
        dtr = sb("dtr", T, 32)
        soft, ln_one = sb("soft", DB * T), sb("ln_one", 1)
        restart = sb("restart", 4 * TSEQ)
        ident, sel = keep["ident"], keep["sel"]

        w_ready, y_stored = sem("w_ready"), sem("y_stored")
        u_ready = [sem(f"u_ready{p}") for p in range(2)]
        work_ready, work_free = sem("work_ready"), [sem(f"work_free{p}") for p in range(2)]
        acc_ready, conv_chain = sem("acc_ready"), sem("conv_chain")
        silu_ready = sem("silu_ready")
        high_ready, mid_ready = sem("high_ready"), sem("mid_ready")
        low_ready, split_ready, dtr_ready = sem("low_ready"), sem("split_ready"), sem("dtr_ready")
        abs_ready, exp_ready, one_plus_ready = sem("abs_ready"), sem("exp_ready"), sem("one_plus_ready")
        lost_ready, ln_ready, dtx_ready = sem("lost_ready"), sem("ln_ready"), sem("dtx_ready")
        decay_ready, dbx_ready = sem("decay_ready"), sem("dbx_ready")
        scan_done, hc_ready, sums_done = sem("scan_done"), sem("hc_ready"), sem("sums_done")
        gx_ready, yg_ready, ones_set, restart_set = sem("gx_ready"), sem("yg_ready"), sem("ones_set"), sem("restart_set")
        ln_one_ready = sem("ln_one_ready")

        win = lambda k, c0: w[:, W_IN + k * 2 * DIN + c0:W_IN + k * 2 * DIN + c0 + 128]
        blk = lambda t, j: t[:, j * T:(j + 1) * T]
        pair = lambda t, h: t[:, 2 * h * T:(2 * h + 2) * T]
        seqs = lambda ap: ap.rearrange("p (s t) -> p s t", t=SEQ)

        class Step:

            def __init__(self, q, o, first=False, last=False):
                self.q, self.o, self.first, self.last = q, o, first, last
                self.par = o % 2

            def at(self, per_step, c):
                return self.q * (2 * per_step) + (per_step * self.o + c)

            def item(self, local):
                return Item(self.q, ITEMS * self.o + ITEMS - 8 + local)

            def bc_last(self, i):
                return self.item(i + (2 if self.first else 0))

            def bc(self, g, i):
                return self.bc_last(4 * (g - GP + 1) + i)

            def out(self, i):
                return self.item(4 + i)

            def out_end(self, i):
                return self.item(6 + i)

            def front(self):
                return Front(self.q, self.o + 1, self.item(6))

        class Item:

            def __init__(self, q, c):
                self.q, self.c, self.slot = q, c, c % 2

            def plus(self, n):
                return Item(self.q, self.c + n)

            def ready(self):
                return self.q * (2 * ITEMS) + (self.c + 1)

            def freed(self):
                return self.q * ITEMS + (self.c // 2 + 2)

            def bank_is_free(self):
                return self.q * ITEMS + (self.c // 2 + 1)

        class Front:

            def __init__(self, q, o, item):
                self.q, self.o, self.par, self.first_item = q, o, o % 2, item

            def at(self, per_step, c):
                return self.q * (2 * per_step) + (per_step * self.o + c)

            def x(self, j):
                return self.first_item.plus(2 * j)

            def z(self, j):
                return self.first_item.plus(2 * j + 1)

            def xp(self):
                return self.first_item.plus(2 * DB)

            def dt(self, j):
                return self.first_item.plus(2 * DB + 1 + j)

            def bc(self, g, i):
                return self.first_item.plus(3 * DB + 1 + 4 * g + i)

            def u_wait(self):
                return self.q * 16 + (self.o // 2 + 1) * 16

        def program(eng, front_prologue, step, before_pass=None, after_pass=None):
            with eng.Fori(0, 2) as m:
                q0 = m * (TILES // 2)
                if before_pass:
                    before_pass(m)
                front_prologue(Front(q0, 0, Item(q0, 0)))
                step(Step(q0, 0, first=True), 0)
                with eng.Fori(0, TILES // 2 - 1) as i:
                    q = m * (TILES // 2) + i
                    step(Step(q, 1), i)
                    step(Step(q, 2), i)
                step(Step(m * (TILES // 2) + (TILES // 2 - 1), 1, last=True), TILES // 2 - 1)

        X_AT, XP_AT, DT_AT, BC_AT, OUT_AT = 5, 16, 19, 25, 3

        with nc.Block() as block:
            @block.sync
            def _(sp):
                def load_u(par, tile):
                    sp.dma_start(u[par][:, :], u_dram[bass.ds(tile, 1)].rearrange("t p n -> p (t n)")).then_inc(u_ready[par], 16)

                def before(m):
                    sp.wait_ge(y_stored, m * (16 * TILES) + ST0)
                    sp.dma_start(w[:, :], w_dram[bass.ds(m, 1)].rearrange("m p n -> p (m n)")).then_inc(w_ready, 16)

                def front(f):
                    load_u(0, 0)

                def store(s, n):
                    tile = sp.snap(s.at(1, n - 1))
                    it = s.out(1) if n == 0 else s.out_end(1)
                    sp.wait_ge(work_free[it.slot], it.freed())
                    sp.dma_start(y_dram[bass.ds(tile, 1)].rearrange("t (c p) f -> p (t c) f", p=TCH),
                                 ytok[:, :].rearrange("p (c f) -> p c f", f=FEAT)).then_inc(y_stored, 16)

                def step(s, i):
                    if not s.last:
                        tile = sp.snap(i * 2 + (s.o + 1))
                        if not s.first:
                            sp.wait_ge(work_ready, s.at(ITEMS, -39))
                        load_u(1 - s.par, tile)
                    if not s.first:
                        store(s, 0)
                    if s.last:
                        store(s, 1)

                sp.sem_inc(y_stored, ST0)
                program(sp, front, step, before)
                sp.wait_ge(y_stored, 2 * 16 * TILES + ST0)

            @block.tensor
            def _(pe):
                def take(item):
                    pe.wait_ge(work_free[item.slot], item.bank_is_free())
                    return work[item.slot]

                def bc_rows(item, n, c):
                    r = c * NST + n
                    nc.tensor.matmul(take(item)[:, 0:T], sel[:, r * 128:(r + 1) * 128], parts[:, :],
                                     start=True, stop=True).then_inc(work_ready, 1)

                def in_proj(f, item, c0):
                    b = take(item)
                    for k in range(2):
                        last = nc.tensor.matmul(b[:, 0:T], win(k, c0), u[f.par][:, k * T:(k + 1) * T], start=(k == 0), stop=(k == 1))
                    last.then_inc(work_ready, 1)

                def x_proj(f):
                    pe.wait_ge(silu_ready, f.at(2, 1))
                    b = take(f.xp())
                    for j in range(DB):
                        last = nc.tensor.matmul(b[0:XPM, 0:T], w[:, W_XP + j * XPM:W_XP + (j + 1) * XPM], blk(x[f.par], j),
                                                start=(j == 0), stop=(j == DB - 1))
                    last.then_inc(work_ready, 1)

                def dt_proj(f, j):
                    b = take(f.dt(j))
                    nc.tensor.matmul(b[:, 0:T], w[0:DTR + 1, W_DT + j * 128:W_DT + (j + 1) * 128], dtr[0:DTR + 1, :],
                                     start=True, stop=True).then_inc(work_ready, 1)

                def bc_group(f, g):
                    for i in range(4):
                        bc_rows(f.bc(g, i), 2 * g + i % 2, i // 2)

                def out_proj(item, i):
                    b = take(item)
                    for h in range(2):
                        c = 2 * i + h
                        for j in range(DB):
                            last = nc.tensor.matmul(b[0:TCH, h * FEAT:(h + 1) * FEAT],
                                                    yg[:, j * T + c * TCH:j * T + (c + 1) * TCH],
                                                    w[:, W_OUT + j * FEAT:W_OUT + (j + 1) * FEAT], start=(j == 0), stop=(j == DB - 1))
                    last.then_inc(work_ready, 1)

                def sums(s, n):
                    pe.wait_ge(hc_ready, s.at(SLOTS, n + 1 + HC0))
                    j, g = n // GP, n % GP
                    if g == 0:
                        pe.wait_ge(gx_ready, s.at(DB, j + 1))
                    for e in range(2):
                        last = nc.tensor.matmul(y_ps[j % 2], ident[:, :], hc[g % RING][:, e * T:(e + 1) * T],
                                                start=(g == 0 and e == 0), stop=(g == GP - 1 and e == 1))
                    last.then_inc(sums_done, 1)

                def front_slot(f, n):
                    if X_AT <= n < X_AT + 2 * DB:
                        if n == X_AT:
                            pe.wait_ge(u_ready[f.par], f.u_wait())
                        j = (n - X_AT) // 2
                        if (n - X_AT) % 2 == 0:
                            in_proj(f, f.x(j), j * 128)
                        else:
                            in_proj(f, f.z(j), DIN + j * 128)
                    if n == XP_AT:
                        x_proj(f)
                    if DT_AT <= n < DT_AT + DB:
                        if n == DT_AT:
                            pe.wait_ge(dtr_ready, f.at(1, 1))
                        dt_proj(f, n - DT_AT)
                    if BC_AT <= n:
                        if n == BC_AT:
                            pe.wait_ge(low_ready, f.at(1, 1))
                            pe.wait_ge(split_ready, f.at(1, 1))
                        bc_group(f, n - BC_AT)

                def before(m):
                    pe.wait_ge(w_ready, m * 16 + 16)

                def front(f):
                    for n in range(SLOTS):
                        front_slot(f, n)

                def step(s, i):
                    for n in range(SLOTS):
                        if n == 0:
                            for e in range(4):
                                bc_rows(s.bc_last(e), 2 * (GP - 1) + e % 2, e // 2)
                        if n == OUT_AT and not s.first:
                            pe.wait_ge(yg_ready, s.at(DB, YG0))
                            out_proj(s.out(0), 0)
                            out_proj(s.out(1), 1)
                        if not s.last:
                            front_slot(s.front(), n)
                        if n > 0:
                            sums(s, n - 1)
                    sums(s, SLOTS - 1)
                    if s.last:
                        pe.wait_ge(yg_ready, s.at(DB, DB + YG0))
                        out_proj(s.out_end(0), 0)
                        out_proj(s.out_end(1), 1)

                for p in range(2):
                    pe.sem_inc(work_free[p], 1)
                program(pe, front, step, before)

            @block.scalar
            def _(act):
                def take(item):
                    act.wait_ge(work_ready, item.ready())
                    return work[item.slot]

                def decays(s, n):
                    j, g = n // GP, n % GP
                    if g == 0 and j % 2 == 0:
                        act.wait_ge(dtx_ready, s.at(8, 4 * (j // 2) + 4))
                    act.wait_ge(hc_ready, s.at(SLOTS, n + 1 + HC0 - 2))
                    for e in range(2):
                        c = W_A + j * NST + 2 * g + e
                        last = nc.scalar.activation(decay[g % 2][:, e * T:(e + 1) * T], blk(dt[s.par], j), ACT.Exp, scale=w[:, c:c + 1])
                    last.then_inc(decay_ready, 1)

                def bc_copy(f_at, items, g):
                    for i in range(4):
                        if i == 0:
                            act.wait_ge(dbx_ready, f_at(SLOTS, SLOTS - GP + g + 1 - SLOTS + BX0))
                        if i == 2:
                            act.wait_ge(hc_ready, f_at(SLOTS, SLOTS - GP + g + 1 - SLOTS + HC0))
                        b = take(items[i])
                        dst = blk(b_all if i < 2 else c_all, 2 * g + i % 2)
                        nc.scalar.copy(dst, b[:, 0:T]).then_inc(work_free[items[i].slot], 1)

                def front_slot(f, n):
                    if X_AT <= n < X_AT + 2 * DB:
                        j = (n - X_AT) // 2
                        if n == X_AT:
                            act.wait_ge(yg_ready, f.at(DB, YG0 - DB))
                        if (n - X_AT) % 2 == 0:
                            nc.scalar.activation(blk(x[f.par], j), take(f.x(j))[:, 0:T], ACT.Identity,
                                                 scale=w[:, W_CW + j * DCONV + DCONV - 1:W_CW + (j + 1) * DCONV],
                                                 bias=w[:, W_CB + j:W_CB + j + 1]).then_inc(acc_ready, 1)
                        else:
                            it = f.z(j)
                            nc.scalar.copy(blk(sz[f.par], j), take(it)[:, 0:T]).then_inc(work_free[it.slot], 1)
                    if n == X_AT + 2 * DB:
                        for it in (f.x(DB - 1), f.z(DB - 1)):
                            act.wait_ge(work_free[it.slot], it.freed())
                        nc.scalar.activation(x[f.par][:, :], x[f.par][:, :], ACT.Silu).then_inc(silu_ready, 1)
                        nc.scalar.activation(sz[f.par][:, :], sz[f.par][:, :], ACT.Silu).then_inc(silu_ready, 1)
                        nc.scalar.preload_act_table_set(EXP_SET)
                    if n == XP_AT:
                        b = take(f.xp())
                        nc.scalar.copy(parts[:, :], b[0:96, 0:T]).then_inc(high_ready, 1)
                        nc.scalar.copy(dtr[0:DTR, :], b[96:96 + DTR, 0:T]).then_inc(dtr_ready, 1)
                    if n == XP_AT + 1:
                        it = f.xp()
                        act.wait_ge(work_free[it.slot], it.freed())
                        nc.scalar.copy(mid[:, :], rest[:, :]).then_inc(mid_ready, 1)
                        act.wait_ge(mid_ready, f.at(1, 1))
                        nc.scalar.copy(parts[32:64, :], mid[32:64, :]).then_inc(split_ready, 1)
                    if DT_AT <= n < DT_AT + DB:
                        j = n - DT_AT
                        h = j // 2
                        nc.scalar.activation(blk(dtx[f.par], j), take(f.dt(j))[:, 0:T], ACT.Abs).then_inc(abs_ready, 1)
                        if j % 2 == 1:
                            e = pair(dtx[f.par], h)
                            act.wait_ge(abs_ready, f.at(DB, j + 1))
                            nc.scalar.activation(e, e, ACT.Exp, scale=-1.0).then_inc(exp_ready, 1)
                            act.wait_ge(exp_ready, f.at(2, h + 1))
                            nc.scalar.activation(pair(soft, h), e, ACT.Identity, bias=1.0).then_inc(one_plus_ready, 1)
                    if n == DT_AT + DB:
                        act.wait_ge(lost_ready, f.at(2, 2))
                        nc.scalar.activation(soft[:, :], soft[:, :], ACT.Ln).then_inc(ln_ready, 1)
                        nc.scalar.preload_act_table_set(EXP_SET)
                    if BC_AT <= n < BC_AT + GP - 2:
                        g = n - BC_AT
                        bc_copy(f.at, [f.bc(g, i) for i in range(4)], g)

                def before(m):
                    act.wait_ge(w_ready, m * 16 + 16)

                def front(f):
                    for n in range(SLOTS):
                        front_slot(f, n)

                def step(s, i):
                    for n in range(SLOTS):
                        decays(s, n)
                        if n == 0:
                            bc_copy(s.at, [s.bc_last(e - 4) for e in range(4)], GP - 2)
                        if n == 1:
                            bc_copy(s.at, [s.bc_last(e) for e in range(4)], GP - 1)
                        if n == OUT_AT + 1 and not s.first:
                            out_copy(s, 0, [s.out(0), s.out(1)])
                        if n > 0 and not s.last:
                            front_slot(s.front(), n - 1)
                    if s.last:
                        out_copy(s, 1, [s.out_end(0), s.out_end(1)])

                def out_copy(s, n, items):
                    act.wait_ge(y_stored, s.at(16, 16 * (n - 1) + ST0))
                    for i in range(2):
                        nc.scalar.copy(ytok[:, i * 512:(i + 1) * 512], take(items[i])[0:TCH, :]).then_inc(work_free[items[i].slot], 1)

                act.wait_ge(ones_set, 1)
                act.wait_ge(ones_set, 2)
                nc.scalar.activation(ln_one[:, :], ln_one[:, :], ACT.Ln).then_inc(ln_one_ready, 1)
                nc.scalar.preload_act_table_set(EXP_SET)
                program(act, front, step, before)

            @block.vector
            def _(dve):
                def conv(f, j):
                    it = f.x(j)
                    dve.wait_ge(acc_ready, f.at(DB, j + 1))
                    for back in range(1, DCONV):
                        c = W_CW + j * DCONV + DCONV - 1 - back
                        dst = seqs(blk(x[f.par], j))[:, :, back:SEQ]
                        src = seqs(work[it.slot][:, 0:T])[:, :, 0:SEQ - back]
                        last = nc.vector.scalar_tensor_tensor(dst, src, w[:, c:c + 1], dst, ALU.mult, ALU.add)
                        if back < DCONV - 1:
                            last.then_inc(conv_chain, 1)
                            dve.wait_ge(conv_chain, f.at(2 * DB, 2 * j + back))
                    last.then_inc(work_free[it.slot], 1)

                def front_slot(f, n):
                    if X_AT <= n < X_AT + 2 * DB and (n - X_AT) % 2 == 0:
                        conv(f, (n - X_AT) // 2)
                    if n == XP_AT:
                        it = f.xp()
                        dve.wait_ge(dtr_ready, f.at(1, 1))
                        nc.vector.tensor_tensor(rest[:, :], work[it.slot][0:96, 0:T], parts[:, :], ALU.subtract).then_inc(work_free[it.slot], 1)
                    if n == XP_AT + 1:
                        dve.wait_ge(mid_ready, f.at(1, 1))
                        nc.vector.tensor_tensor(parts[64:96, :], rest[64:96, :], mid[64:96, :], ALU.subtract).then_inc(low_ready, 1)
                    if DT_AT <= n < DT_AT + DB:
                        j = n - DT_AT
                        it = f.dt(j)
                        dve.wait_ge(abs_ready, f.at(DB, j + 1))
                        nc.vector.tensor_scalar(blk(dt[f.par], j), work[it.slot][:, 0:T], 0.0, ln_one[:, 0:1],
                                                ALU.max, ALU.subtract).then_inc(work_free[it.slot], 1)
                        if j % 2 == 1:
                            h = j // 2
                            e = pair(dtx[f.par], h)
                            dve.wait_ge(one_plus_ready, f.at(2, h + 1))
                            nc.vector.scalar_tensor_tensor(e, pair(soft, h), 1.0, e, ALU.subtract, ALU.subtract).then_inc(lost_ready, 1)

                def gate(s, j):
                    dve.wait_ge(sums_done, s.at(SLOTS, GP * (j + 1) + SD0))
                    dve.wait_ge(yg_ready, s.at(DB, j - 1 + YG0))
                    par = s.par
                    nc.vector.scalar_tensor_tensor(gx[j % 2][:, :], blk(x[par], j), w[:, W_D + j:W_D + j + 1], y_ps[j % 2],
                                                   ALU.mult, ALU.add).then_inc(gx_ready, 1)

                def gate_before(s):
                    dve.wait_ge(sums_done, s.at(SLOTS, SD0))
                    dve.wait_ge(yg_ready, s.at(DB, -2 + YG0))
                    j = DB - 1
                    nc.vector.scalar_tensor_tensor(gx[j % 2][:, :], blk(x[1 - s.par], j), w[:, W_D + j:W_D + j + 1], y_ps[j % 2],
                                                   ALU.mult, ALU.add).then_inc(gx_ready, 1)

                def recur(s, n):
                    j, g = n // GP, n % GP
                    h = decay[g % 2]
                    dve.wait_ge(decay_ready, s.at(SLOTS, n + 1))
                    dve.wait_ge(dbx_ready, s.at(SLOTS, n + 1 + BX0))
                    nc.vector.tensor_tensor_scan(h, h, dbx[g % RING][:, :], 0.0, ALU.mult, ALU.add).then_inc(scan_done, 1)
                    if j == 0:
                        it = s.bc(g, 3)
                        dve.wait_ge(work_free[it.slot], it.freed())
                    dve.wait_ge(sums_done, s.at(SLOTS, n + 1))
                    dve.wait_ge(scan_done, s.at(SLOTS, n + 1 + RING))
                    nc.vector.tensor_tensor(hc[g % RING][:, :], h, c_all[:, 2 * g * T:(2 * g + 2) * T], ALU.mult).then_inc(hc_ready, 1)

                def front(f):
                    for n in range(SLOTS):
                        front_slot(f, n)

                def before(m):
                    dve.wait_ge(w_ready, m * 16 + 16)

                def step(s, i):
                    for n in range(SLOTS):
                        recur(s, n)
                        if n == 1 and not s.first:
                            gate_before(s)
                        if n % GP == 1 and n > GP:
                            gate(s, n // GP - 1)
                        if n > 0 and not s.last:
                            front_slot(s.front(), n - 1)
                    if s.last:
                        gate(s, DB - 1)

                nc.vector.memset(dtr[:, :], 1.0).then_inc(ones_set, 1)
                nc.vector.memset(ln_one[:, :], 1.0).then_inc(ones_set, 1)
                dve.wait_ge(ln_one_ready, 1)
                dve.sem_inc(sums_done, SD0)
                dve.sem_inc(hc_ready, HC0)
                dve.sem_inc(gx_ready, GR0)
                program(dve, front, step, before)

            @block.gpsimd
            def _(pool):
                def make_dtx(f, h):
                    d, dx = pair(dt[f.par], h), pair(dtx[f.par], h)
                    pool.wait_ge(ln_ready, f.at(1, 1))
                    it = f.dt(2 * h + 1)
                    pool.wait_ge(work_free[it.slot], it.freed())
                    nc.gpsimd.tensor_tensor(d, d, pair(soft, h), ALU.add).then_inc(dtx_ready, 1)
                    pool.wait_ge(dtx_ready, f.at(8, 4 * h + 1))
                    nc.gpsimd.tensor_tensor(d, d, dx, ALU.subtract).then_inc(dtx_ready, 1)
                    pool.wait_ge(dtx_ready, f.at(8, 4 * h + 2))
                    nc.gpsimd.tensor_tensor(dx, d, pair(x[f.par], h), ALU.mult).then_inc(dtx_ready, 1)
                    pool.wait_ge(dtx_ready, f.at(8, 4 * h + 3))
                    nc.gpsimd.tensor_tensor(seqs(d)[:, :, 0], restart[:, 0:2 * TSEQ], restart[:, 2 * TSEQ:4 * TSEQ],
                                            ALU.mult).then_inc(dtx_ready, 1)

                def gated(s, j, par, value):
                    pool.wait_ge(gx_ready, value)
                    nc.gpsimd.tensor_tensor(blk(yg, j), gx[j % 2][:, :], blk(sz[par], j), ALU.mult).then_inc(yg_ready, 1)

                def make_dbx(s, n):
                    j, g = n // GP, n % GP
                    if g == 0 and j % 2 == 0:
                        pool.wait_ge(dtx_ready, s.at(8, 4 * (j // 2) + 4))
                    if j == 0:
                        it = s.bc(g, 1)
                        pool.wait_ge(work_free[it.slot], it.freed())
                    pool.wait_ge(scan_done, s.at(SLOTS, n + 1))
                    nc.gpsimd.tensor_tensor(view(dbx[g % RING], 0, [[T, 2], [1, T]]), view(dtx[s.par], j * T, [[0, 2], [1, T]]),
                                            view(b_all, 2 * g * T, [[T, 2], [1, T]]), ALU.mult).then_inc(dbx_ready, 1)

                def front(f):
                    for h in range(2):
                        make_dtx(f, h)

                LEAD = 4

                def step(s, i):
                    for n in range(SLOTS):
                        make_dbx(s, n)
                        if n == LEAD + 1 and not s.first:
                            gated(s, DB - 1, 1 - s.par, s.at(DB, GR0))
                        if n % GP == LEAD + 2 and n > GP:
                            j = n // GP - 1
                            if j == 0:
                                pool.wait_ge(work_ready, s.at(ITEMS, ITEMS - 2))
                            gated(s, j, s.par, s.at(DB, j + 1 + GR0))
                        if not s.last and n in (DT_AT + LEAD + 5, DT_AT + LEAD + 7):
                            make_dtx(s.front(), (n - DT_AT - LEAD - 5) // 2)
                    if s.last:
                        gated(s, DB - 1, s.par, s.at(DB, DB + GR0))

                nc.gpsimd.memset(restart[:, 0:2 * TSEQ], RESTART)
                nc.gpsimd.memset(restart[:, 2 * TSEQ:4 * TSEQ], 1.0).then_inc(restart_set, 1)
                pool.wait_ge(restart_set, 1)
                pool.sem_inc(dbx_ready, BX0)
                pool.sem_inc(scan_done, RING)
                pool.sem_inc(yg_ready, YG0)
                program(pool, front, step)


def finish(nc, x_in, y_dram, k_dram, cat_dram, out, keep):
    with ExitStack() as ctx:
        sb = lambda name, cols: ctx.enter_context(nc.sbuf_tensor(name, [128, cols], fp32))
        sem = lambda name: ctx.enter_context(nc.semaphore(name))
        ps = ctx.enter_context(nc.psum_tensor("fin_ps", [128, 8 * 512], fp32))
        src = [sb(f"src{i}", 6 * T) for i in range(TPB)]
        res = [sb(f"res{i}", 2 * T) for i in range(TPB)]
        cat_t, maps, now = sb("cat_tt", 4 * CH), sb("maps", BATCH * KCOLS), sb("now", KCOLS)
        fixed, src_ready = sem("fixed"), [sem(f"src_ready{i}") for i in range(TPB)]
        now_ready, made, taken = sem("now_ready"), sem("made"), sem("taken")
        stored = [sem(f"out_stored{i}") for i in range(TPB)]
        y_img = y_dram.rearrange("(m b t) n f -> m b (t n f)", m=2, b=BATCH).rearrange("m b (k p n) -> m b p k n", k=2, p=128)

        with nc.Block() as block:
            @block.sync
            def _(sp):
                sp.dma_start(cat_t[:, :], cat_dram).then_inc(fixed, 16)
                sp.dma_start(maps[:, :].rearrange("p (b n) -> p b n", b=BATCH), k_dram.rearrange("b p n -> p b n")).then_inc(fixed, 16)
                sp.sem_inc(made, TPB)
                with sp.Fori(0, BATCH) as b:
                    for i in range(TPB):
                        sp.wait_ge(made, b * TPB + (i + 1))
                        s = src[i][:, :].rearrange("p (k n) -> p k n", k=6)
                        for m in range(2):
                            sp.dma_start(s[:, 2 * m:2 * m + 2, :], y_img[m][bass.ds(b, 1)].rearrange("b p k n -> p (b k) n")[:, :, i * T:(i + 1) * T]).then_inc(src_ready[i], 16)
                        sp.dma_start(s[:, 4:6, :], x_in[bass.ds(b, 1)].rearrange("b (k p) n -> p (b k) n", p=128)[:, :, i * T:(i + 1) * T]).then_inc(src_ready[i], 16)

            @block.vector
            def _(dve):
                dve.sem_inc(taken, TPB)
                dve.wait_ge(fixed, 32)
                with dve.Fori(0, BATCH) as b:
                    dve.wait_ge(made, b * TPB + TPB)
                    dve.wait_ge(taken, b * TPB + TPB)
                    nc.vector.tensor_copy(now[:, :], maps[:, bass.ds(b * KCOLS, KCOLS)]).then_inc(now_ready, 1)

            @block.tensor
            def _(pe):
                pe.wait_ge(fixed, 32)
                with pe.Fori(0, BATCH) as b:
                    pe.wait_ge(now_ready, b + 1)
                    for i in range(TPB):
                        pe.wait_ge(src_ready[i], b * 48 + 48)
                        back = 4 if i >= 4 else (7 if i == 3 else 3)
                        pe.wait_ge(taken, b * TPB + (i + 1 - back + TPB))
                        for oc in range(2):
                            o = ((i % 4) * 2 + oc) * 512
                            for k in range(6):
                                w = cat_t[:, k * CH + oc * 128:k * CH + (oc + 1) * 128] if k < 4 else \
                                    now[:, (k - 4) * CH + oc * 128:(k - 4) * CH + (oc + 1) * 128]
                                last = nc.tensor.matmul(ps[:, o:o + T], w, src[i][:, k * T:(k + 1) * T], start=(k == 0), stop=(k == 5))
                        last.then_inc(made, 1)

            @block.scalar
            def _(act):
                for i in range(TPB):
                    act.sem_inc(stored[i], 16)
                with act.Fori(0, BATCH) as b:
                    for i in range(TPB):
                        act.wait_ge(made, b * TPB + (i + 1 + TPB))
                        act.wait_ge(stored[i], b * 16 + 16)
                        for oc in range(2):
                            o = ((i % 4) * 2 + oc) * 512
                            last = nc.scalar.activation(res[i][:, oc * T:(oc + 1) * T], ps[:, o:o + T], ACT.Identity,
                                                        bias=now[:, 2 * CH + oc:2 * CH + oc + 1])
                        last.then_inc(taken, 1)
                        act.wait_ge(taken, b * TPB + (i + 1 + TPB))
                        act.dma_start(out[bass.ds(b, 1)].rearrange("b (k p) n -> p (b k) n", p=128)[:, :, i * T:(i + 1) * T],
                                      res[i][:, :].rearrange("p (k n) -> p k n", k=2)).then_inc(stored[i], 16)
                for i in range(TPB):
                    act.wait_ge(stored[i], 16 * BATCH + 16)


def build(nc, a, out):
    x_in = a["x"].rearrange("b c h w -> b c (h w)")
    out = out.rearrange("b c h w -> b c (h w)")
    w_dram = nc.dram_tensor("w_scratch", [2, 128, W_COLS], fp32).ap()
    cat_dram = nc.dram_tensor("cat_scratch", [128, 4 * CH], fp32).ap()
    u_dram = nc.dram_tensor("u_scratch", [TILES, 128, 2 * T], fp32).ap()
    k_dram = nc.dram_tensor("k_scratch", [BATCH, 128, KCOLS], fp32).ap()
    y_dram = nc.dram_tensor("y_scratch", [2 * TILES, T, FEAT], fp32).ap()
    with ExitStack() as ctx:
        keep = {}
        for name, rows, cols, dtype in (("ident", 128, 128, fp32), ("sel", 96, 2 * NST * 128, bf16)):
            keep[name] = ctx.enter_context(nc.sbuf_tensor(name, [rows, cols], dtype))
        keep["kn_free"] = ctx.enter_context(nc.semaphore("kn_free"))
        with ExitStack() as early:
            for name, cols in (("wpg", 512), ("wrec", 256), ("wtheta", 256), ("btheta", 1), ("btrep", 128), ("pgbias", 256),
                               ("invn", CH + 2), ("cst", CH + 2), ("catb", 2), ("id2", 2 * CH)):
                keep[name] = early.enter_context(nc.sbuf_tensor(name, [128, cols], fp32))
            prepare(nc, a, w_dram, cat_dram, keep)
            attention(nc, x_in, u_dram, k_dram, keep)
        mambas(nc, u_dram, w_dram, y_dram, keep)
        finish(nc, x_in, y_dram, k_dram, cat_dram, out, keep)


_INS = ["x"] + ["L0_conv_" + n for n in ("w_theta", "b_theta", "w_phi", "b_phi", "w_g", "b_g", "w_rec", "b_rec", "bn_gamma",
                                         "bn_beta", "bn_mean", "bn_var")] + \
       ["L1_conv_" + n + m for m in "12" for n in ("in_proj_w", "conv_w", "conv_b", "x_proj_w", "dt_proj_w", "dt_proj_b",
                                                   "A_log", "D", "out_proj_w")] + ["L1_conv_cat_conv_w", "L1_conv_cat_conv_b"]


def kernel(**inputs):
    import ml_dtypes
    import numpy as np
    import concourse.bacc as bacc
    from concourse.bass_utils import run_bass_kernel_spmd

    nc = bacc.Bacc("TRN2", target_bir_lowering=False, num_devices=1)
    arrays = {n: np.ascontiguousarray(inputs[n]) for n in _INS}
    arrays["ident"] = np.eye(128, dtype=np.float32)
    pick = np.zeros((96, 2 * NST, 128), dtype=ml_dtypes.bfloat16)
    for p in range(96):
        pick[p, p % (2 * NST), :] = 1
    arrays["sel"] = pick.reshape(96, -1)
    aps = {n: nc.dram_tensor(f"in_{n}", v.shape, mybir.dt.from_np(v.dtype), kind="ExternalInput").ap() for n, v in arrays.items()}
    out = nc.dram_tensor("out_0", (BATCH, CH, SIDE, SIDE), fp32, kind="ExternalOutput").ap()
    build(nc, aps, out)
    r = run_bass_kernel_spmd(nc, [{f"in_{n}": v for n, v in arrays.items()}], core_ids=[0])
    return r.results[0]["out_0"]
```

```python
from contextlib import ExitStack

import concourse.bass as bass
from concourse import mybir

BATCH, CH, SIDE = 4, 256, 56
NPOS = SIDE * SIDE
CMID = 128
DIN, NST, DTR, DCONV = 512, 16, 16, 4
SEQ, FEAT = SIDE, CH
TSEQ = 8
T = TSEQ * SEQ
TPB = NPOS // T
TILES = BATCH * TPB
DB = DIN // 128
GP = NST // 2
SLOTS = DB * GP
XPM = 2 * NST + DTR
TCH = T // 4
HALF = NPOS // 28
NBLK = NPOS // 64

W_IN, W_OUT, W_XP = 0, 2 * 2 * DIN, 2 * 2 * DIN + DB * FEAT
W_DT = W_XP + DB * XPM
W_CW = W_DT + DIN
W_CB = W_CW + DB * DCONV
W_D = W_CB + DB
W_A = W_D + DB
W_COLS = W_A + DB * NST
KCOLS = 2 * CH + 2

BN_EPS = 1e-5
RESTART, A_TOP = 1e28, -1e-25

fp32 = mybir.dt.float32
ALU, ACT = mybir.AluOpType, mybir.ActivationFunctionType
EXP_SET = "exp_and_others"

ITEMS = 2 + 2 * DB + 1 + DB

BX_RING, HC_RING = 8, 4
BX0, HC0, SD0, YG0, ST0 = SLOTS + GP - 1, SLOTS + GP - 1, HC_RING, 2 * DB, 16


def view(t, offset, dims, parts=128, first=0):
    row = t.shape[1]
    return bass.AP(tensor=t, offset=first * row + offset, ap=[[row, parts]] + [list(d) for d in dims])


def prepare(nc, a, w_dram, cat_dram, keep):
    with ExitStack() as ctx:
        sb = lambda name, cols, parts=128: ctx.enter_context(nc.sbuf_tensor(name, [parts, cols], fp32))
        sem = lambda name: ctx.enter_context(nc.semaphore(name))
        ps = ctx.enter_context(nc.psum_tensor("prep_ps", [128, 8 * 512], fp32))
        raw_in = [sb(f"raw_in{m}", 8 * 256) for m in range(2)]
        raw_out = [sb(f"raw_out{m}", 2 * 512) for m in range(2)]
        raw_xp = [sb(f"raw_xp{m}", 512) for m in range(2)]
        raw_dt = [sb(f"raw_dt{m}", DB * DTR) for m in range(2)]
        raw_a = [sb(f"raw_a{m}", DB * NST) for m in range(2)]
        pack = [sb(f"pack{m}", W_COLS) for m in range(2)]
        raw_cat, raw_pg, raw_rec = sb("raw_cat", 2 * 512), sb("raw_pg", 2 * 256), sb("raw_rec", 2 * 128)
        cat_t = sb("cat_t", 4 * 256)
        W2 = CH + 2
        bn = sb("bn", 5 * W2)
        root = sb("root", 2 * W2)
        ident, wpg, wrec, invn, cst = keep["ident"], keep["wpg"], keep["wrec"], keep["invn"], keep["cst"]
        loaded, cleared, placed = sem("prep_loaded"), sem("prep_cleared"), sem("prep_placed")
        turned, copied = sem("prep_turned"), sem("prep_copied")
        a_exp, bn_root, chain, stored = sem("prep_a_exp"), sem("prep_root"), sem("prep_chain"), sem("prep_stored")

        jobs = []
        for m in range(2):
            for k in range(2):
                for h in range(2):
                    src = [raw_in[m][:, (4 * h + r) * 256 + k * 128:(4 * h + r) * 256 + (k + 1) * 128] for r in range(4)]
                    o = W_IN + k * 2 * DIN + h * 512
                    jobs.append((src, 128, 128, pack[m][:, o:o + 512]))
            for jj in range(2):
                src = [raw_out[m][:, fc * 512 + j * 128:fc * 512 + (j + 1) * 128] for j in (2 * jj, 2 * jj + 1) for fc in range(2)]
                jobs.append((src, 128, 128, pack[m][:, W_OUT + jj * 512:W_OUT + (jj + 1) * 512]))
            src = [raw_xp[m][0:XPM, j * 128:(j + 1) * 128] for j in range(DB)]
            jobs.append((src, 128, XPM, pack[m][:, W_XP:W_XP + DB * XPM]))
            src = [raw_dt[m][:, j * DTR:(j + 1) * DTR] for j in range(DB)]
            jobs.append((src, DTR, 128, pack[m][0:DTR, W_DT:W_DT + DIN]))
        for jj in range(2):
            src = [raw_cat[:, oc * 512 + j * 128:oc * 512 + (j + 1) * 128] for j in (2 * jj, 2 * jj + 1) for oc in range(2)]
            jobs.append((src, 128, 128, cat_t[:, jj * 512:(jj + 1) * 512]))
        src = [raw_pg[:, w * 256 + k * 128:w * 256 + (k + 1) * 128] for k in range(2) for w in range(2)]
        jobs.append((src, 128, 128, wpg[:, :]))
        jobs.append(([raw_rec[:, oc * 128:(oc + 1) * 128] for oc in range(2)], 128, 128, wrec[:, :]))

        loads = [(ident[:, :], a["ident"])]
        for m in range(2):
            n = str(m + 1)
            loads.append((raw_in[m][:, :].rearrange("p (r c) -> p r c", r=8), a["L1_conv_in_proj_w" + n].rearrange("(r p) c -> p r c", p=128)))
            loads.append((raw_out[m][:, :].rearrange("p (r c) -> p r c", r=2), a["L1_conv_out_proj_w" + n].rearrange("(r p) c -> p r c", p=128)))
            xp = a["L1_conv_x_proj_w" + n]
            loads.append((raw_xp[m][0:2 * NST, :], xp[DTR:DTR + 2 * NST, :]))
            loads.append((raw_xp[m][2 * NST:XPM, :], xp[0:DTR, :]))
            loads.append((raw_dt[m][:, :].rearrange("p (j c) -> p j c", j=DB), a["L1_conv_dt_proj_w" + n].rearrange("(j p) c -> p j c", p=128)))
            loads.append((raw_a[m][:, :].rearrange("p (j c) -> p j c", j=DB), a["L1_conv_A_log" + n].rearrange("(j p) c -> p j c", p=128)))
        loads.append((raw_cat[:, :].rearrange("p (r c) -> p r c", r=2), a["L1_conv_cat_conv_w"].rearrange("(r p) c -> p r c", p=128)))
        loads.append((raw_pg[:, 0:256], a["L0_conv_w_phi"]))
        loads.append((raw_pg[:, 256:512], a["L0_conv_w_g"]))
        loads.append((raw_rec[:, :].rearrange("p (r c) -> p r c", r=2), a["L0_conv_w_rec"].rearrange("(r p) c -> p r c", p=128)))
        loads.append((keep["wtheta"][:, :], a["L0_conv_w_theta"]))
        loads.append((keep["btheta"][:, :], a["L0_conv_b_theta"].unsqueeze(1)))
        loads.append((keep["pgbias"][:, 0:128], a["L0_conv_b_phi"].partition_broadcast(128)))
        loads.append((keep["pgbias"][:, 128:256], a["L0_conv_b_g"].partition_broadcast(128)))
        loads.append((keep["catb"][:, :], a["L1_conv_cat_conv_b"].rearrange("(o p) -> p o", p=128)))
        for i, n in enumerate(("bn_gamma", "bn_var", "bn_beta", "bn_mean", "b_rec")):
            loads.append((bn[:, i * W2:i * W2 + CH], a["L0_conv_" + n].partition_broadcast(128)))
            loads.append((bn[:, i * W2 + CH:(i + 1) * W2], a["L0_conv_" + n].rearrange("(o p) -> p o", p=128)))
        direct = []
        for m in range(2):
            n = str(m + 1)
            direct.append((pack[m][:, W_CW:W_CW + DB * DCONV].rearrange("p (j c) -> p j c", j=DB), a["L1_conv_conv_w" + n].rearrange("(j p) c -> p j c", p=128)))
            direct.append((pack[m][:, W_CB:W_CB + DB], a["L1_conv_conv_b" + n].rearrange("(j p) -> p j", p=128)))
            direct.append((pack[m][:, W_D:W_D + DB], a["L1_conv_D" + n].rearrange("(j p) -> p j", p=128)))
            direct.append((pack[m][DTR:DTR + 1, W_DT:W_DT + DIN], a["L1_conv_dt_proj_b" + n].unsqueeze(0)))

        with nc.Block() as block, nc.allow_non_contiguous_dma(reason="small per-channel vectors"):
            @block.sync
            def _(sp):
                for dst, src in loads:
                    sp.dma_start(dst, src).then_inc(loaded, 16)
                sp.wait_ge(cleared, 1)
                for dst, src in direct:
                    sp.dma_start(dst, src).then_inc(placed, 16)
                sp.wait_ge(placed, 16 * len(direct))
                sp.wait_ge(copied, len(jobs) + 2)
                for m in range(2):
                    sp.dma_start(w_dram[m], pack[m][:, :]).then_inc(stored, 16)
                sp.dma_start(cat_dram, cat_t[:, :]).then_inc(stored, 16)
                sp.wait_ge(stored, 48)

            @block.scalar
            def _(act):
                act.wait_ge(loaded, 16 * len(loads))
                act.wait_ge(chain, 1)
                nc.scalar.activation(root[:, 0:W2], bn[:, W2:2 * W2], ACT.Sqrt).then_inc(bn_root, 1)
                for m in range(2):
                    nc.scalar.activation(raw_a[m][:, :], raw_a[m][:, :], ACT.Exp).then_inc(a_exp, 1)

            @block.tensor
            def _(pe):
                pe.wait_ge(loaded, 16 * len(loads))
                for i, (srcs, rows, cols, _) in enumerate(jobs):
                    if i >= 4:
                        pe.wait_ge(copied, i - 3)
                    for r, s in enumerate(srcs):
                        o = (i % 4) * 512 + r * cols
                        p = s.shape[0]
                        last = nc.tensor.transpose(ps[0:rows, o:o + cols], s, ident[0:p, 0:p])
                    last.then_inc(turned, 1)

            @block.vector
            def _(dve):
                for m in range(2):
                    last = nc.vector.memset(pack[m][:, W_DT:W_DT + DIN], 0.0)
                last.then_inc(cleared, 1)
                dve.wait_ge(loaded, 16 * len(loads))
                gamma, var, beta, mean, brec = (bn[:, i * W2:(i + 1) * W2] for i in range(5))
                nc.vector.tensor_scalar_add(var, var, BN_EPS).then_inc(chain, 1)
                dve.wait_ge(cleared, 1)
                for i, (srcs, rows, cols, dst) in enumerate(jobs):
                    dve.wait_ge(turned, i + 1)
                    o = (i % 4) * 512
                    nc.vector.tensor_copy(dst, ps[0:rows, o:o + len(srcs) * cols]).then_inc(copied, 1)
                for m in range(2):
                    dve.wait_ge(a_exp, m + 1)
                    nc.vector.tensor_scalar(pack[m][:, W_A:W_A + DB * NST], raw_a[m][:, :], -1.0, A_TOP, ALU.mult, ALU.min).then_inc(copied, 1)
                count = [1]

                def link(ins):
                    count[0] += 1
                    ins.then_inc(chain, 1)
                    dve.wait_ge(chain, count[0])

                r, s = root[:, 0:W2], root[:, W2:2 * W2]
                dve.wait_ge(bn_root, 1)
                link(nc.vector.reciprocal(r, r))
                link(nc.vector.tensor_tensor(s, r, r, ALU.mult))
                link(nc.vector.tensor_tensor(s, s, var, ALU.mult))
                link(nc.vector.tensor_scalar(s, s, -0.5, 1.5, ALU.mult, ALU.add))
                link(nc.vector.tensor_tensor(r, r, s, ALU.mult))
                link(nc.vector.tensor_tensor(r, r, gamma, ALU.mult))
                link(nc.vector.tensor_tensor(s, brec, mean, ALU.subtract))
                link(nc.vector.tensor_tensor(s, s, r, ALU.mult))
                link(nc.vector.tensor_tensor(cst[:, :], s, beta, ALU.add))
                link(nc.vector.tensor_scalar_mul(invn[:, :], r, 1.0 / NPOS))
                link(nc.vector.tensor_tensor(keep["catb"][:, :], keep["catb"][:, :], cst[:, CH:CH + 2], ALU.add))
                link(nc.vector.memset(keep["id2"][:, :], 0.0))
                for k in range(2):
                    link(nc.vector.tensor_copy(keep["id2"][:, k * CH + k * 128:k * CH + (k + 1) * 128], ident[:, :]))
                nc.vector.tensor_copy(keep["btrep"][:, :], keep["btheta"][:, :].to_broadcast([128, 128])).then_inc(chain, 1)


def attention(nc, x_in, u_dram, k_dram, keep):
    PAIRS = 14
    UT = 13
    with ExitStack() as ctx:
        sb = lambda name, cols, parts=128: ctx.enter_context(nc.sbuf_tensor(name, [parts, cols], fp32))
        sem = lambda name: ctx.enter_context(nc.semaphore(name))
        ps = ctx.enter_context(nc.psum_tensor("att_ps", [128, 8 * 512], fp32))
        bank = lambda i: ps[:, i * 512:(i + 1) * 512]
        xb = [sb(f"xb{o}", 2 * NPOS) for o in range(2)]
        ub = [sb(f"ub{o}", 2 * NPOS) for o in range(2)]
        pg = [sb(f"pg{i}", 512) for i in range(2)]
        mt_sb, r_sb = sb("mt_sb", 128), sb("r_sb", CH)
        kn, kp, kb = sb("kn", KCOLS), sb("kp", 2 * CH), sb("kb", CH)
        x_ready = [sem(f"x_ready{o}") for o in range(2)]
        pg_ready, pg_taken, mt_step = sem("pg_ready"), sem("pg_taken"), sem("mt_step")
        k_pe, k_dve, k_stored = sem("k_pe"), sem("k_dve"), sem("k_stored")
        ut_ready, ut_taken = sem("ut_ready"), sem("ut_taken")
        u_stored = [sem(f"u_stored{o}") for o in range(2)]
        wpg, wrec, wtheta = keep["wpg"], keep["wrec"], keep["wtheta"]

        def group(cls, n):
            ks = [cls + 16 * n + 4 * i for i in range(4)]
            return [k for k in ks if k + 1 < NBLK]

        ut_items = [(cls, group(cls, n)) for n in range(3) for cls in (0, 2, 1, 3)] + [("edge", [])]
        assert len(ut_items) == UT

        def token_view(o, k, r, count, parts, first):
            at = []
            for rr in (r, r + 2):
                q = (rr + k) % 4
                if first:
                    q -= 1
                    at.append((q // 2) * NPOS + (NBLK * rr + k - q - 1) // 4)
                else:
                    at.append((q // 2) * NPOS + (NBLK * rr + k - q) // 4)
            return view(ub[o], at[0], [[1, count], [at[1] - at[0], 2], [NBLK, 64]], parts, first)

        with nc.Block() as block:
            @block.sync
            def _(sp):
                sp.sem_inc(ut_ready, 2 * UT)
                with sp.Fori(0, 2) as it:
                    for o in range(2):
                        b = sp.snap(it * 2 + o)
                        sp.wait_ge(ut_ready, it * (2 * UT) + (UT * (o - 1) + 2 * UT))
                        sp.dma_start(xb[o][:, :].rearrange("p (k n) -> p k n", k=2),
                                     x_in[bass.ds(b, 1)].rearrange("b (k p) n -> p (b k) n", p=128)).then_inc(x_ready[o], 16)

            @block.scalar
            def _(act):
                for o in range(2):
                    act.sem_inc(u_stored[o], 16)
                with act.Fori(0, 2) as it:
                    for o in range(2):
                        act.wait_ge(k_dve, it * 8 + (4 * o + 3))
                        act.dma_start(k_dram[bass.ds(it * 2 + o, 1)].rearrange("b p n -> p (b n)"), kn[:, :]).then_inc(k_stored, 16)
                        act.wait_ge(ut_taken, it * (2 * UT) + (UT * (o + 1) + 2))
                        for i in range(TPB):
                            act.dma_start(u_dram[bass.ds((it * 2 + o) * TPB + i, 1)].rearrange("t p (k n) -> p (t k) n", k=2),
                                          ub[o][:, :].rearrange("p (k n) -> p k n", k=2)[:, :, i * T:(i + 1) * T]).then_inc(u_stored[o], 16)
                act.wait_ge(k_stored, 16 * BATCH)
                for o in range(2):
                    act.wait_ge(u_stored[o], 16 + 2 * 16 * TPB)

            @block.tensor
            def _(pe):
                pe.sem_inc(pg_taken, 2)
                pe.sem_inc(ut_taken, 2)
                with pe.Fori(0, 2) as it:
                    for o in range(2):
                        P = lambda c: it * (2 * PAIRS) + (PAIRS * o + c)
                        U = lambda c: it * (2 * UT) + (UT * o + c)

                        def add_pair(i):
                            pe.wait_ge(pg_taken, P(i + 3))
                            for h in range(2):
                                s = pg[i % 2]
                                last = nc.tensor.matmul(bank(2)[:, 0:CMID], s[0:HALF, h * 256 + 128:h * 256 + 256],
                                                        s[0:HALF, h * 256:h * 256 + 128],
                                                        start=(i == 0 and h == 0), stop=(i == PAIRS - 1 and h == 1))
                            last.then_inc(mt_step, 1)

                        pe.wait_ge(x_ready[o], it * 16 + 16)
                        for i in range(PAIRS):
                            pe.wait_ge(pg_taken, P(i + 1))
                            for h in range(2):
                                n0 = (2 * i + h) * HALF
                                for k in range(2):
                                    last = nc.tensor.matmul(bank(i % 2)[0:HALF, h * 256:(h + 1) * 256],
                                                            xb[o][:, k * NPOS + n0:k * NPOS + n0 + HALF],
                                                            wpg[:, k * 256:(k + 1) * 256], start=(k == 0), stop=(k == 1))
                            last.then_inc(pg_ready, 1)
                            if i:
                                add_pair(i - 1)
                        add_pair(PAIRS - 1)
                        pe.wait_ge(k_dve, it * 8 + (4 * o + 1))
                        nc.tensor.matmul(bank(3)[:, 0:CH], mt_sb[:, :], wrec[:, :], start=True, stop=True).then_inc(k_pe, 1)
                        pe.wait_ge(k_dve, it * 8 + (4 * o + 2))
                        for k in range(2):
                            nc.tensor.matmul(bank(4)[:, k * CH:(k + 1) * CH], wtheta[:, k * 128:(k + 1) * 128], r_sb[:, :],
                                             start=True, stop=True)
                        nc.tensor.matmul(bank(5)[:, 0:CH], keep["btrep"][:, :], r_sb[:, :], start=True, stop=True)
                        for k in range(2):
                            last = nc.tensor.matmul(bank(5)[:, CH + k:CH + k + 1], r_sb[:, k * 128:(k + 1) * 128],
                                                    keep["btheta"][:, :], start=True, stop=True)
                        last.then_inc(k_pe, 1)
                        pe.wait_ge(k_dve, it * 8 + (4 * o + 4))
                        for i, (cls, ks) in enumerate(ut_items):
                            pe.wait_ge(ut_taken, U(i + 1))
                            b = bank(6 + (i + o) % 2)
                            if cls == "edge":
                                for rows, n0, par in ((0, 64 * (NBLK - 1), 0), (64, 0, 1)):
                                    for k2 in range(2):
                                        last = nc.tensor.matmul(b[rows:rows + 64, rows * 2:rows * 2 + 128],
                                                                xb[o][:, k2 * NPOS + n0:k2 * NPOS + n0 + 64],
                                                                kp[:, k2 * CH + par * 128:k2 * CH + par * 128 + 128],
                                                                start=(k2 == 0), stop=(k2 == 1))
                            for j, kk in enumerate(ks):
                                par = kk % 2
                                for k2 in range(2):
                                    n0 = k2 * NPOS + 64 * kk
                                    last = nc.tensor.matmul(b[:, j * 128:(j + 1) * 128], xb[o][:, n0:n0 + 128],
                                                            kp[:, k2 * CH + par * 128:k2 * CH + par * 128 + 128],
                                                            start=(k2 == 0), stop=(k2 == 1))
                            last.then_inc(ut_ready, 1)

            @block.vector
            def _(dve):
                dve.sem_inc(mt_step, 2)
                with dve.Fori(0, 2) as it:
                    for o in range(2):
                        P = lambda c: it * (2 * PAIRS) + (PAIRS * o + c)
                        K = lambda c: it * 8 + (4 * o + c)
                        for i in range(PAIRS):
                            dve.wait_ge(pg_ready, P(i + 1))
                            dve.wait_ge(mt_step, P(i + 1))
                            nc.vector.tensor_tensor(view(pg[i % 2], 0, [[256, 2], [1, 256]], HALF),
                                                    bank(i % 2)[0:HALF, :].rearrange("p (h c) -> p h c", h=2),
                                                    view(keep["pgbias"], 0, [[0, 2], [1, 256]], HALF), ALU.add).then_inc(pg_taken, 1)
                        dve.wait_ge(mt_step, P(PAIRS + 2))
                        nc.vector.tensor_copy(mt_sb[:, :], bank(2)[:, 0:CMID]).then_inc(k_dve, 1)
                        dve.wait_ge(k_pe, it * 4 + (2 * o + 1))
                        nc.vector.tensor_tensor(r_sb[:, :], bank(3)[:, 0:CH], keep["invn"][:, 0:CH], ALU.mult).then_inc(k_dve, 1)
                        dve.wait_ge(k_pe, it * 4 + (2 * o + 2))
                        if o == 0:
                            dve.wait_ge(keep["kn_free"], it * 1 + 1)
                        else:
                            dve.wait_ge(k_stored, it * 32 + 16)
                        nc.vector.tensor_tensor(kn[:, 0:2 * CH], bank(4), keep["id2"][:, :], ALU.add)
                        order = [[64, 2], [128, 2], [1, 64]]
                        nc.vector.tensor_tensor(view(kb, 0, order), view(ps, 5 * 512, [[2, 2], [1, 2], [4, 64]]),
                                                view(keep["cst"], 0, [[2, 2], [1, 2], [4, 64]]), ALU.add)
                        nc.vector.tensor_tensor(kn[:, 2 * CH:2 * CH + 2], bank(5)[:, CH:CH + 2], keep["catb"][:, :], ALU.add).then_inc(k_dve, 1)
                        dve.wait_ge(k_dve, K(3))
                        for k in range(2):
                            last = nc.vector.tensor_copy(view(kp, k * CH, order), view(kn, k * CH, [[2, 2], [1, 2], [4, 64]]))
                        last.then_inc(k_dve, 1)
                        dve.wait_ge(u_stored[o], it * (16 * TPB) + 16)
                        for i, (cls, ks) in enumerate(ut_items):
                            dve.wait_ge(ut_ready, it * (2 * UT) + (UT * o + i + 1 + 2 * UT))
                            if i == 0:
                                dve.wait_ge(k_dve, K(4))
                            b = (6 + (i + o) % 2) * 512
                            if cls == "edge":
                                nc.vector.tensor_tensor(token_view(o, NBLK - 1, 0, 1, 64, 0), view(ps, b, [[128, 1], [64, 2], [1, 64]], 64),
                                                        view(kb, 0, [[0, 1], [64, 2], [1, 64]], 64), ALU.add)
                                nc.vector.tensor_tensor(token_view(o, 0, 1, 1, 64, 64), view(ps, b + 128, [[128, 1], [64, 2], [1, 64]], 64, 64),
                                                        view(kb, 128, [[0, 1], [64, 2], [1, 64]], 64, 64), ALU.add).then_inc(ut_taken, 1)
                            else:
                                par = cls % 2
                                nc.vector.tensor_tensor(token_view(o, ks[0], par, len(ks), 128, 0),
                                                        view(ps, b, [[128, len(ks)], [64, 2], [1, 64]]),
                                                        view(kb, par * 128, [[0, len(ks)], [64, 2], [1, 64]]), ALU.add).then_inc(ut_taken, 1)

            @block.gpsimd
            def _(pool):
                pool.sem_inc(keep["kn_free"], 1)
                pool.wait_ge(k_stored, 32)
                pool.sem_inc(keep["kn_free"], 1)


def mambas(nc, u_dram, w_dram, y_dram, bc_dram, keep):
    with ExitStack() as ctx:
        sb = lambda name, cols, parts=128, dt=fp32: ctx.enter_context(nc.sbuf_tensor(name, [parts, cols], dt))
        sem = lambda name: ctx.enter_context(nc.semaphore(name))
        ps = ctx.enter_context(nc.psum_tensor("mamba_ps", [128, 8 * 512], fp32))
        bank = lambda i: ps[:, i * 512:(i + 1) * 512]
        decay = [ps[:, i * 1024:i * 1024 + 2 * T] for i in range(2)]
        y_ps = [bank(4)[:, 0:T], bank(5)[:, 0:T]]
        work = [bank(6), bank(7)]

        w = sb("w", W_COLS)
        u = [sb(f"u{p}", 2 * T) for p in range(2)]
        x = [sb(f"x{p}", DB * T) for p in range(2)]
        sz = [sb(f"sz{p}", DB * T) for p in range(2)]
        dt = [sb(f"dt{p}", DB * T) for p in range(2)]
        dtx = [sb(f"dtx{p}", DB * T) for p in range(2)]
        b_all, c_all = sb("b_all", NST * T), sb("c_all", NST * T)
        dbx = [sb(f"dbx{i}", 2 * T) for i in range(BX_RING)]
        hc = [sb(f"hc{i}", 2 * T) for i in range(HC_RING)]
        skip = sb("skip", DB * 128)
        yg = sb("yg", DB * T)
        ytok = sb("ytok", 4 * FEAT, TCH)
        bc_rows = sb("bc_rows", T, 2 * NST)
        dtr = sb("dtr", T, 32)
        soft, neg_ln_one = sb("soft", DB * T), sb("neg_ln_one", 1)
        restart = sb("restart", 4 * TSEQ)
        ident = keep["ident"]

        w_ready, y_stored = sem("w_ready"), sem("y_stored")
        u_ready = [sem(f"u_ready{p}") for p in range(2)]
        work_ready, work_free = sem("work_ready"), [sem(f"work_free{p}") for p in range(2)]
        acc_ready, conv_chain = sem("acc_ready"), sem("conv_chain")
        silu_ready = sem("silu_ready")
        rows_ready, rows_stored = sem("rows_ready"), sem("rows_stored")
        b_loaded, c_loaded = ([sem(f"{n}_loaded{g}") for g in range(GP)] for n in "bc")
        abs_ready, exp_ready, one_plus_ready = sem("abs_ready"), sem("exp_ready"), sem("one_plus_ready")
        lost_ready, ln_ready, dtx_ready = sem("lost_ready"), sem("ln_ready"), sem("dtx_ready")
        decay_ready, dbx_ready = sem("decay_ready"), sem("dbx_ready")
        scan_done, hc_ready, sums_done = sem("scan_done"), sem("hc_ready"), sem("sums_done")
        skip_ready, yg_ready, ones_set, restart_set = sem("skip_ready"), sem("yg_ready"), sem("ones_set"), sem("restart_set")
        ln_one_ready, ln_chain = sem("ln_one_ready"), sem("ln_chain")

        win = lambda k, c0: w[:, W_IN + k * 2 * DIN + c0:W_IN + k * 2 * DIN + c0 + 128]
        blk = lambda t, j: t[:, j * T:(j + 1) * T]
        pair = lambda t, h: t[:, 2 * h * T:(2 * h + 2) * T]
        seqs = lambda ap: ap.rearrange("p (s t) -> p s t", t=SEQ)

        class Step:

            def __init__(self, q, o, first=False, last=False):
                self.q, self.o, self.first, self.last = q, o, first, last
                self.par = o % 2

            def at(self, per_step, c):
                return self.q * (2 * per_step) + (per_step * self.o + c)

            def item(self, local):
                return Item(self.q, ITEMS * self.o + ITEMS - 4 + local)

            def out(self, i):
                return self.item(i)

            def out_end(self, i):
                return self.item(2 + i)

            def front(self):
                return Front(self.q, self.o + 1, self.item(2))

        class Item:

            def __init__(self, q, c):
                self.q, self.c, self.slot = q, c, c % 2

            def plus(self, n):
                return Item(self.q, self.c + n)

            def ready(self):
                return self.q * (2 * ITEMS) + (self.c + 1)

            def freed(self):
                return self.q * ITEMS + (self.c // 2 + 2)

            def bank_is_free(self):
                return self.q * ITEMS + (self.c // 2 + 1)

        class Front:

            def __init__(self, q, o, item):
                self.q, self.o, self.par, self.first_item = q, o, o % 2, item

            def at(self, per_step, c):
                return self.q * (2 * per_step) + (per_step * self.o + c)

            def x(self, j):
                return self.first_item.plus(2 * j)

            def z(self, j):
                return self.first_item.plus(2 * j + 1)

            def xp(self):
                return self.first_item.plus(2 * DB)

            def dt(self, j):
                return self.first_item.plus(2 * DB + 1 + j)

            def u_wait(self):
                return self.q * 16 + (self.o // 2 + 1) * 16

        def program(eng, front_prologue, step, before_pass=None, after_pass=None):
            with eng.Fori(0, 2) as m:
                q0 = m * (TILES // 2)
                if before_pass:
                    before_pass(m)
                front_prologue(Front(q0, 0, Item(q0, 0)))
                step(Step(q0, 0, first=True), 0)
                with eng.Fori(0, TILES // 2 - 1) as i:
                    q = m * (TILES // 2) + i
                    step(Step(q, 1), i)
                    step(Step(q, 2), i)
                step(Step(m * (TILES // 2) + (TILES // 2 - 1), 1, last=True), TILES // 2 - 1)

        OUT_AT, COPY_AT, X_AT, XP_AT, DT_AT = 3, 6, 7, 17, 19
        DTX_EARLY, DTX_LATE = (28, 29, 30, 31), (2, 4, 6, 7)

        with nc.Block() as block:
            @block.sync
            def _(sp):
                def load_u(par, tile):
                    sp.dma_start(u[par][:, :], u_dram[bass.ds(tile, 1)].rearrange("t p n -> p (t n)")).then_inc(u_ready[par], 16)

                def before(m):
                    sp.wait_ge(y_stored, m * (16 * TILES) + ST0)
                    sp.dma_start(w[:, :], w_dram[bass.ds(m, 1)].rearrange("m p n -> p (m n)")).then_inc(w_ready, 16)

                def spread_bc(f):
                    sp.wait_ge(rows_ready, f.at(1, 1))
                    for r in (0, NST):
                        sp.dma_start(bc_dram[f.par, r:r + NST], bc_rows[r:r + NST, :]).then_inc(rows_stored, 16)
                    sp.wait_ge(rows_stored, f.at(32, 32))
                    flat = bc_dram[f.par].rearrange("r t -> (r t)")
                    for g in range(GP):
                        for dst, r, used, credit, arrived in ((b_all, 0, dbx_ready, BX0, b_loaded), (c_all, NST, hc_ready, HC0, c_loaded)):
                            sp.wait_ge(used, f.at(SLOTS, g + 1 - GP + credit))
                            src = flat[(r + 2 * g) * T:(r + 2 * g + 2) * T].partition_broadcast(128)
                            sp.dma_start(dst[:, 2 * g * T:(2 * g + 2) * T], src).then_inc(arrived[g], 16)

                def front(f):
                    load_u(0, 0)
                    spread_bc(f)

                def store(s, n):
                    tile = sp.snap(s.at(1, n - 1))
                    it = s.out(1) if n == 0 else s.out_end(1)
                    sp.wait_ge(work_free[it.slot], it.freed())
                    sp.dma_start(y_dram[bass.ds(tile, 1)].rearrange("t (c p) f -> p (t c) f", p=TCH),
                                 ytok[:, :].rearrange("p (c f) -> p c f", f=FEAT)).then_inc(y_stored, 16)

                def step(s, i):
                    if not s.last:
                        tile = sp.snap(i * 2 + (s.o + 1))
                        if not s.first:
                            sp.wait_ge(work_ready, s.at(ITEMS, -7))
                        load_u(1 - s.par, tile)
                    if not s.first:
                        store(s, 0)
                    if s.last:
                        store(s, 1)
                    else:
                        spread_bc(s.front())

                sp.sem_inc(y_stored, ST0)
                program(sp, front, step, before)
                sp.wait_ge(y_stored, 2 * 16 * TILES + ST0)

            @block.tensor
            def _(pe):
                def take(item):
                    pe.wait_ge(work_free[item.slot], item.bank_is_free())
                    return work[item.slot]

                def in_proj(f, item, c0):
                    b = take(item)
                    for k in range(2):
                        last = nc.tensor.matmul(b[:, 0:T], win(k, c0), u[f.par][:, k * T:(k + 1) * T], start=(k == 0), stop=(k == 1))
                    last.then_inc(work_ready, 1)

                def x_proj(f):
                    pe.wait_ge(silu_ready, f.at(2, 1))
                    b = take(f.xp())
                    for j in range(DB):
                        last = nc.tensor.matmul(b[0:XPM, 0:T], w[:, W_XP + j * XPM:W_XP + (j + 1) * XPM], blk(x[f.par], j),
                                                start=(j == 0), stop=(j == DB - 1))
                    last.then_inc(work_ready, 1)

                def dt_proj(f, j):
                    b = take(f.dt(j))
                    nc.tensor.matmul(b[:, 0:T], w[0:DTR + 1, W_DT + j * 128:W_DT + (j + 1) * 128], dtr[0:DTR + 1, :],
                                     start=True, stop=True).then_inc(work_ready, 1)

                def out_proj(item, c):
                    h = c % 2
                    b = take(item) if h == 0 else work[item.slot]
                    for j in range(DB):
                        last = nc.tensor.matmul(b[0:TCH, h * FEAT:(h + 1) * FEAT],
                                                yg[:, j * T + c * TCH:j * T + (c + 1) * TCH],
                                                w[:, W_OUT + j * FEAT:W_OUT + (j + 1) * FEAT], start=(j == 0), stop=(j == DB - 1))
                    if h == 1:
                        last.then_inc(work_ready, 1)

                def sums(s, n):
                    j, g = n // GP, n % GP
                    if g == 0:
                        pe.wait_ge(yg_ready, s.at(DB, j - 1 + YG0))
                        nc.tensor.matmul(y_ps[j % 2], skip[:, j * 128:(j + 1) * 128], blk(x[s.par], j), start=True, stop=False)
                    pe.wait_ge(hc_ready, s.at(SLOTS, n + 1 + HC0))
                    for e in range(2):
                        last = nc.tensor.matmul(y_ps[j % 2], ident[:, :], hc[g % HC_RING][:, e * T:(e + 1) * T],
                                                start=False, stop=(g == GP - 1 and e == 1))
                    last.then_inc(sums_done, 1)

                def front_slot(f, n):
                    if X_AT <= n < X_AT + 2 * DB:
                        if n == X_AT:
                            pe.wait_ge(u_ready[f.par], f.u_wait())
                        j = (n - X_AT) // 2
                        if (n - X_AT) % 2 == 0:
                            in_proj(f, f.x(j), j * 128)
                        else:
                            in_proj(f, f.z(j), DIN + j * 128)
                    if n == XP_AT:
                        x_proj(f)
                    if DT_AT <= n < DT_AT + DB:
                        if n == DT_AT:
                            it = f.xp()
                            pe.wait_ge(work_free[it.slot], it.freed())
                        dt_proj(f, n - DT_AT)

                def before(m):
                    pe.wait_ge(w_ready, m * 16 + 16)
                    pe.wait_ge(skip_ready, m * DB + DB)

                def front(f):
                    for n in range(SLOTS):
                        front_slot(f, n)

                def step(s, i):
                    for n in range(SLOTS):
                        if OUT_AT <= n < OUT_AT + 4 and not s.first:
                            if n == OUT_AT:
                                pe.wait_ge(yg_ready, s.at(DB, YG0))
                            out_proj(s.out((n - OUT_AT) // 2), n - OUT_AT)
                        if not s.last:
                            front_slot(s.front(), n)
                        if n > 0:
                            sums(s, n - 1)
                    sums(s, SLOTS - 1)
                    if s.last:
                        pe.wait_ge(yg_ready, s.at(DB, DB + YG0))
                        for c in range(4):
                            out_proj(s.out_end(c // 2), c)

                for p in range(2):
                    pe.sem_inc(work_free[p], 1)
                program(pe, front, step, before)

            @block.scalar
            def _(act):
                def take(item):
                    act.wait_ge(work_ready, item.ready())
                    return work[item.slot]

                def decays(s, n):
                    j, g = n // GP, n % GP
                    if g == 0 and j % 2 == 0:
                        act.wait_ge(dtx_ready, s.at(8, 4 * (j // 2) + 4))
                    act.wait_ge(hc_ready, s.at(SLOTS, n + 1 + HC0 - 2))
                    for e in range(2):
                        c = W_A + j * NST + 2 * g + e
                        last = nc.scalar.activation(decay[g % 2][:, e * T:(e + 1) * T], blk(dt[s.par], j), ACT.Exp, scale=w[:, c:c + 1])
                    last.then_inc(decay_ready, 1)

                def front_slot(f, n):
                    if X_AT <= n < X_AT + 2 * DB:
                        j = (n - X_AT) // 2
                        if n == X_AT:
                            act.wait_ge(yg_ready, f.at(DB, YG0 - DB))
                        if (n - X_AT) % 2 == 0:
                            nc.scalar.activation(blk(x[f.par], j), take(f.x(j))[:, 0:T], ACT.Identity,
                                                 scale=w[:, W_CW + j * DCONV + DCONV - 1:W_CW + (j + 1) * DCONV],
                                                 bias=w[:, W_CB + j:W_CB + j + 1]).then_inc(acc_ready, 1)
                        else:
                            it = f.z(j)
                            nc.scalar.copy(blk(sz[f.par], j), take(it)[:, 0:T]).then_inc(work_free[it.slot], 1)
                    if n == X_AT + 2 * DB:
                        for it in (f.x(DB - 1), f.z(DB - 1)):
                            act.wait_ge(work_free[it.slot], it.freed())
                        nc.scalar.activation(x[f.par][:, :], x[f.par][:, :], ACT.Silu).then_inc(silu_ready, 1)
                        nc.scalar.activation(sz[f.par][:, :], sz[f.par][:, :], ACT.Silu).then_inc(silu_ready, 1)
                        nc.scalar.preload_act_table_set(EXP_SET)
                    if n == XP_AT:
                        b = take(f.xp())
                        nc.scalar.copy(bc_rows[:, :], b[0:2 * NST, 0:T]).then_inc(rows_ready, 1)
                        nc.scalar.copy(dtr[0:DTR, :], b[2 * NST:XPM, 0:T]).then_inc(work_free[f.xp().slot], 1)
                    if DT_AT <= n < DT_AT + DB:
                        j = n - DT_AT
                        h = j // 2
                        it = f.dt(j)
                        v = take(it)[:, 0:T]
                        nc.scalar.activation(blk(dtx[f.par], j), v, ACT.Abs).then_inc(abs_ready, 1)
                        nc.scalar.activation(blk(dt[f.par], j), v, ACT.Relu).then_inc(work_free[it.slot], 1)
                        if j % 2 == 1:
                            e = pair(dtx[f.par], h)
                            act.wait_ge(abs_ready, f.at(DB, j + 1))
                            nc.scalar.activation(e, e, ACT.Exp, scale=-1.0).then_inc(exp_ready, 1)
                            act.wait_ge(exp_ready, f.at(2, h + 1))
                            nc.scalar.activation(pair(soft, h), e, ACT.Identity, bias=1.0).then_inc(one_plus_ready, 1)
                    if n == DT_AT + DB:
                        act.wait_ge(lost_ready, f.at(2, 2))
                        nc.scalar.activation(soft[:, :], soft[:, :], ACT.Ln).then_inc(ln_chain, 1)
                        nc.scalar.preload_act_table_set(EXP_SET)
                    if n == DT_AT + DB + 1:
                        act.wait_ge(ln_chain, f.at(1, 2))
                        nc.scalar.activation(soft[:, :], soft[:, :], ACT.Identity, bias=neg_ln_one[:, 0:1]).then_inc(ln_ready, 1)

                def before(m):
                    act.wait_ge(w_ready, m * 16 + 16)

                def front(f):
                    for n in range(SLOTS):
                        front_slot(f, n)

                def step(s, i):
                    for n in range(SLOTS):
                        decays(s, n)
                        if n in (COPY_AT, COPY_AT + 2) and not s.first:
                            i = (n - COPY_AT) // 2
                            out_copy(s, 0, i, s.out(i))
                        if n > 0 and not s.last:
                            front_slot(s.front(), n - 1)
                    if s.last:
                        for i in range(2):
                            out_copy(s, 1, i, s.out_end(i))

                def out_copy(s, n, i, item):
                    if i == 0:
                        act.wait_ge(y_stored, s.at(16, 16 * (n - 1) + ST0))
                    nc.scalar.copy(ytok[:, i * 512:(i + 1) * 512], take(item)[0:TCH, :]).then_inc(work_free[item.slot], 1)

                act.wait_ge(ones_set, 1)
                act.wait_ge(ones_set, 2)
                nc.scalar.activation(neg_ln_one[:, :], neg_ln_one[:, :], ACT.Ln).then_inc(ln_chain, 1)
                act.wait_ge(ln_chain, 1)
                nc.scalar.activation(neg_ln_one[:, :], neg_ln_one[:, :], ACT.Identity, scale=-1.0).then_inc(ln_one_ready, 1)
                act.wait_ge(ln_one_ready, 1)
                nc.scalar.preload_act_table_set(EXP_SET)
                program(act, front, step, before)

            @block.vector
            def _(dve):
                def conv(f, j):
                    it = f.x(j)
                    dve.wait_ge(acc_ready, f.at(DB, j + 1))
                    for back in range(1, DCONV):
                        c = W_CW + j * DCONV + DCONV - 1 - back
                        dst = seqs(blk(x[f.par], j))[:, :, back:SEQ]
                        src = seqs(work[it.slot][:, 0:T])[:, :, 0:SEQ - back]
                        last = nc.vector.scalar_tensor_tensor(dst, src, w[:, c:c + 1], dst, ALU.mult, ALU.add)
                        if back < DCONV - 1:
                            last.then_inc(conv_chain, 1)
                            dve.wait_ge(conv_chain, f.at(2 * DB, 2 * j + back))
                    last.then_inc(work_free[it.slot], 1)

                def front_slot(f, n):
                    if X_AT <= n < X_AT + 2 * DB and (n - X_AT) % 2 == 0:
                        conv(f, (n - X_AT) // 2)
                    if DT_AT <= n < DT_AT + DB and (n - DT_AT) % 2 == 1:
                        h = (n - DT_AT) // 2
                        e = pair(dtx[f.par], h)
                        dve.wait_ge(one_plus_ready, f.at(2, h + 1))
                        nc.vector.scalar_tensor_tensor(e, pair(soft, h), 1.0, e, ALU.subtract, ALU.subtract).then_inc(lost_ready, 1)

                def gate(s, j, par, sums):
                    dve.wait_ge(sums_done, sums)
                    nc.vector.tensor_tensor(blk(yg, j), y_ps[j % 2], blk(sz[par], j), ALU.mult).then_inc(yg_ready, 1)

                def recur(s, n):
                    j, g = n // GP, n % GP
                    h = decay[g % 2]
                    dve.wait_ge(decay_ready, s.at(SLOTS, n + 1))
                    dve.wait_ge(dbx_ready, s.at(SLOTS, n + 1 + BX0))
                    nc.vector.tensor_tensor_scan(h, h, dbx[g % BX_RING][:, :], 0.0, ALU.mult, ALU.add).then_inc(scan_done, 1)
                    if j == 0:
                        dve.wait_ge(c_loaded[g], s.at(16, 16))
                    dve.wait_ge(sums_done, s.at(SLOTS, n + 1))
                    dve.wait_ge(scan_done, s.at(SLOTS, n + 1 + BX_RING))
                    nc.vector.tensor_tensor(hc[g % HC_RING][:, :], h, c_all[:, 2 * g * T:(2 * g + 2) * T], ALU.mult).then_inc(hc_ready, 1)

                def front(f):
                    for n in range(SLOTS):
                        front_slot(f, n)

                def before(m):
                    dve.wait_ge(w_ready, m * 16 + 16)
                    for j in range(DB):
                        nc.vector.tensor_scalar_mul(skip[:, j * 128:(j + 1) * 128], ident[:, :], w[:, W_D + j:W_D + j + 1]).then_inc(skip_ready, 1)

                def step(s, i):
                    for n in range(SLOTS):
                        recur(s, n)
                        if n == 2 and not s.first:
                            gate(s, DB - 1, 1 - s.par, s.at(SLOTS, SD0))
                        if n % GP == 2 and n > GP:
                            j = n // GP - 1
                            if j == 0 and not s.first:
                                dve.wait_ge(work_ready, s.at(ITEMS, ITEMS - 2))
                            gate(s, j, s.par, s.at(SLOTS, GP * (j + 1) + SD0))
                        if n > 0 and not s.last:
                            front_slot(s.front(), n - 1)
                    if s.last:
                        gate(s, DB - 1, s.par, s.at(SLOTS, SLOTS + SD0))

                nc.vector.memset(dtr[:, :], 1.0).then_inc(ones_set, 1)
                nc.vector.memset(neg_ln_one[:, :], 1.0).then_inc(ones_set, 1)
                dve.sem_inc(sums_done, SD0)
                dve.sem_inc(hc_ready, HC0)
                dve.sem_inc(yg_ready, YG0)
                program(dve, front, step, before)

            @block.gpsimd
            def _(pool):
                def make_dtx(f, k):
                    h, part = k // 4, k % 4
                    d, dx = pair(dt[f.par], h), pair(dtx[f.par], h)
                    if part == 0:
                        pool.wait_ge(ln_ready, f.at(1, 1))
                        ins = nc.gpsimd.tensor_tensor(d, d, pair(soft, h), ALU.add)
                    else:
                        pool.wait_ge(dtx_ready, f.at(8, k))
                        if part == 1:
                            ins = nc.gpsimd.tensor_tensor(d, d, dx, ALU.subtract)
                        elif part == 2:
                            ins = nc.gpsimd.tensor_tensor(dx, d, pair(x[f.par], h), ALU.mult)
                        else:
                            ins = nc.gpsimd.tensor_tensor(seqs(d)[:, :, 0], restart[:, 0:2 * TSEQ], restart[:, 2 * TSEQ:4 * TSEQ], ALU.mult)
                    ins.then_inc(dtx_ready, 1)

                def make_dbx(s, n):
                    j, g = n // GP, n % GP
                    if g == 0 and j % 2 == 0:
                        pool.wait_ge(dtx_ready, s.at(8, 4 * (j // 2) + 4))
                    if j == 0:
                        pool.wait_ge(b_loaded[g], s.at(16, 16))
                    pool.wait_ge(scan_done, s.at(SLOTS, n + 1))
                    nc.gpsimd.tensor_tensor(view(dbx[g % BX_RING], 0, [[T, 2], [1, T]]), view(dtx[s.par], j * T, [[0, 2], [1, T]]),
                                            view(b_all, 2 * g * T, [[T, 2], [1, T]]), ALU.mult).then_inc(dbx_ready, 1)

                def front(f):
                    for k in range(4):
                        make_dtx(f, k)

                def step(s, i):
                    for n in range(SLOTS):
                        make_dbx(s, n)
                        if n in DTX_LATE:
                            make_dtx(s, 4 + DTX_LATE.index(n))
                        if not s.last and n in DTX_EARLY:
                            make_dtx(s.front(), DTX_EARLY.index(n))

                nc.gpsimd.memset(restart[:, 0:2 * TSEQ], RESTART)
                nc.gpsimd.memset(restart[:, 2 * TSEQ:4 * TSEQ], 1.0).then_inc(restart_set, 1)
                pool.wait_ge(restart_set, 1)
                pool.sem_inc(dbx_ready, BX0)
                pool.sem_inc(scan_done, BX_RING)
                program(pool, front, step)


def finish(nc, x_in, y_dram, k_dram, cat_dram, out, keep):
    with ExitStack() as ctx:
        sb = lambda name, cols: ctx.enter_context(nc.sbuf_tensor(name, [128, cols], fp32))
        sem = lambda name: ctx.enter_context(nc.semaphore(name))
        ps = ctx.enter_context(nc.psum_tensor("fin_ps", [128, 8 * 512], fp32))
        src = [sb(f"src{i}", 6 * T) for i in range(TPB)]
        res = [sb(f"res{i}", 2 * T) for i in range(TPB)]
        cat_t, maps, now = sb("cat_tt", 4 * CH), sb("maps", BATCH * KCOLS), sb("now", KCOLS)
        fixed, src_ready = sem("fixed"), [sem(f"src_ready{i}") for i in range(TPB)]
        now_ready, made, taken = sem("now_ready"), sem("made"), sem("taken")
        stored = [sem(f"out_stored{i}") for i in range(TPB)]
        y_img = y_dram.rearrange("(m b t) n f -> m b (t n f)", m=2, b=BATCH).rearrange("m b (k p n) -> m b p k n", k=2, p=128)

        with nc.Block() as block:
            @block.sync
            def _(sp):
                sp.dma_start(cat_t[:, :], cat_dram).then_inc(fixed, 16)
                sp.dma_start(maps[:, :].rearrange("p (b n) -> p b n", b=BATCH), k_dram.rearrange("b p n -> p b n")).then_inc(fixed, 16)
                sp.sem_inc(made, TPB)
                with sp.Fori(0, BATCH) as b:
                    for i in range(TPB):
                        sp.wait_ge(made, b * TPB + (i + 1))
                        s = src[i][:, :].rearrange("p (k n) -> p k n", k=6)
                        for m in range(2):
                            sp.dma_start(s[:, 2 * m:2 * m + 2, :], y_img[m][bass.ds(b, 1)].rearrange("b p k n -> p (b k) n")[:, :, i * T:(i + 1) * T]).then_inc(src_ready[i], 16)
                        sp.dma_start(s[:, 4:6, :], x_in[bass.ds(b, 1)].rearrange("b (k p) n -> p (b k) n", p=128)[:, :, i * T:(i + 1) * T]).then_inc(src_ready[i], 16)

            @block.vector
            def _(dve):
                dve.sem_inc(taken, TPB)
                dve.wait_ge(fixed, 32)
                with dve.Fori(0, BATCH) as b:
                    dve.wait_ge(made, b * TPB + TPB)
                    dve.wait_ge(taken, b * TPB + TPB)
                    nc.vector.tensor_copy(now[:, :], maps[:, bass.ds(b * KCOLS, KCOLS)]).then_inc(now_ready, 1)

            @block.tensor
            def _(pe):
                pe.wait_ge(fixed, 32)
                with pe.Fori(0, BATCH) as b:
                    pe.wait_ge(now_ready, b + 1)
                    for i in range(TPB):
                        pe.wait_ge(src_ready[i], b * 48 + 48)
                        back = 4 if i >= 4 else (7 if i == 3 else 3)
                        pe.wait_ge(taken, b * TPB + (i + 1 - back + TPB))
                        for oc in range(2):
                            o = ((i % 4) * 2 + oc) * 512
                            for k in range(6):
                                w = cat_t[:, k * CH + oc * 128:k * CH + (oc + 1) * 128] if k < 4 else \
                                    now[:, (k - 4) * CH + oc * 128:(k - 4) * CH + (oc + 1) * 128]
                                last = nc.tensor.matmul(ps[:, o:o + T], w, src[i][:, k * T:(k + 1) * T], start=(k == 0), stop=(k == 5))
                        last.then_inc(made, 1)

            @block.scalar
            def _(act):
                for i in range(TPB):
                    act.sem_inc(stored[i], 16)
                with act.Fori(0, BATCH) as b:
                    for i in range(TPB):
                        act.wait_ge(made, b * TPB + (i + 1 + TPB))
                        act.wait_ge(stored[i], b * 16 + 16)
                        for oc in range(2):
                            o = ((i % 4) * 2 + oc) * 512
                            last = nc.scalar.activation(res[i][:, oc * T:(oc + 1) * T], ps[:, o:o + T], ACT.Identity,
                                                        bias=now[:, 2 * CH + oc:2 * CH + oc + 1])
                        last.then_inc(taken, 1)
                        act.wait_ge(taken, b * TPB + (i + 1 + TPB))
                        act.dma_start(out[bass.ds(b, 1)].rearrange("b (k p) n -> p (b k) n", p=128)[:, :, i * T:(i + 1) * T],
                                      res[i][:, :].rearrange("p (k n) -> p k n", k=2)).then_inc(stored[i], 16)
                for i in range(TPB):
                    act.wait_ge(stored[i], 16 * BATCH + 16)


def build(nc, a, out):
    x_in = a["x"].rearrange("b c h w -> b c (h w)")
    out = out.rearrange("b c h w -> b c (h w)")
    w_dram = nc.dram_tensor("w_scratch", [2, 128, W_COLS], fp32).ap()
    cat_dram = nc.dram_tensor("cat_scratch", [128, 4 * CH], fp32).ap()
    u_dram = nc.dram_tensor("u_scratch", [TILES, 128, 2 * T], fp32).ap()
    k_dram = nc.dram_tensor("k_scratch", [BATCH, 128, KCOLS], fp32).ap()
    y_dram = nc.dram_tensor("y_scratch", [2 * TILES, T, FEAT], fp32).ap()
    bc_dram = nc.dram_tensor("bc_scratch", [2, 2 * NST, T], fp32).ap()
    with ExitStack() as ctx:
        keep = {"ident": ctx.enter_context(nc.sbuf_tensor("ident", [128, 128], fp32))}
        keep["kn_free"] = ctx.enter_context(nc.semaphore("kn_free"))
        with ExitStack() as early:
            for name, cols in (("wpg", 512), ("wrec", 256), ("wtheta", 256), ("btheta", 1), ("btrep", 128), ("pgbias", 256),
                               ("invn", CH + 2), ("cst", CH + 2), ("catb", 2), ("id2", 2 * CH)):
                keep[name] = early.enter_context(nc.sbuf_tensor(name, [128, cols], fp32))
            prepare(nc, a, w_dram, cat_dram, keep)
            attention(nc, x_in, u_dram, k_dram, keep)
        mambas(nc, u_dram, w_dram, y_dram, bc_dram, keep)
        finish(nc, x_in, y_dram, k_dram, cat_dram, out, keep)


_INS = ["x"] + ["L0_conv_" + n for n in ("w_theta", "b_theta", "w_phi", "b_phi", "w_g", "b_g", "w_rec", "b_rec", "bn_gamma",
                                         "bn_beta", "bn_mean", "bn_var")] + \
       ["L1_conv_" + n + m for m in "12" for n in ("in_proj_w", "conv_w", "conv_b", "x_proj_w", "dt_proj_w", "dt_proj_b",
                                                   "A_log", "D", "out_proj_w")] + ["L1_conv_cat_conv_w", "L1_conv_cat_conv_b"]


def kernel(**inputs):
    import numpy as np
    import concourse.bacc as bacc
    from concourse.bass_utils import run_bass_kernel_spmd

    nc = bacc.Bacc("TRN2", target_bir_lowering=False, num_devices=1)
    arrays = {n: np.ascontiguousarray(inputs[n]) for n in _INS}
    arrays["ident"] = np.eye(128, dtype=np.float32)
    aps = {n: nc.dram_tensor(f"in_{n}", v.shape, mybir.dt.from_np(v.dtype), kind="ExternalInput").ap() for n, v in arrays.items()}
    out = nc.dram_tensor("out_0", (BATCH, CH, SIDE, SIDE), fp32, kind="ExternalOutput").ap()
    build(nc, aps, out)
    r = run_bass_kernel_spmd(nc, [{f"in_{n}": v for n, v in arrays.items()}], core_ids=[0])
    return r.results[0]["out_0"]
```

```python
from contextlib import ExitStack

import concourse.bass as bass
from concourse import mybir

BATCH, CH, SIDE = 4, 256, 56
NPOS = SIDE * SIDE
CMID = 128
DIN, NST, DTR, DCONV = 512, 16, 16, 4
SEQ, FEAT = SIDE, CH
TSEQ = 8
T = TSEQ * SEQ
TPB = NPOS // T
TILES = BATCH * TPB
DB = DIN // 128
GP = NST // 2
SLOTS = DB * GP
XPM = 2 * NST + DTR
TCH = T // 4
HALF = NPOS // 28
NBLK = NPOS // 64

W_IN, W_OUT, W_XP = 0, 2 * 2 * DIN, 2 * 2 * DIN + DB * FEAT
W_DT = W_XP + DB * XPM
W_CW = W_DT + DIN
W_CB = W_CW + DB * DCONV
W_D = W_CB + DB
W_A = W_D + DB
W_COLS = W_A + DB * NST
KCOLS = 2 * CH + 2

BN_EPS = 1e-5
RESTART, A_TOP = 1e28, -1e-25

fp32 = mybir.dt.float32
ALU, ACT = mybir.AluOpType, mybir.ActivationFunctionType
EXP_SET = "exp_and_others"

SCHEDULE = {
    "x0": (0, 3, 2), "x1": (2, 5, 4), "out0": (3, 7, None), "x2": (5, 8, 7), "out1": (6, 10, None), "x3": (8, 11, 10),
    "z0": (10, 12, None), "xp": (13, 15, None), "dt0": (15, 16, None), "dt1": (16, 17, 17), "dt2": (17, 18, None),
    "dt3": (18, 19, 19), "z1": (20, 23, None), "z2": (22, 25, None), "z3": (24, 26, None),
}
ITEMS = len(SCHEDULE)
SILU_X_AT, LN_AT, LN_LESS_AT, SILU_Z_AT = 13, 21, 23, 28
GATE_AT = (13, 21, 28)
DTX_EARLY, DTX_LATE = (28, 29, 30, 31), (2, 4, 6, 7)
OUTS = [n for n in SCHEDULE if n.startswith("out")]
FRONT = [n for n in SCHEDULE if not n.startswith("out")]


def due(engine, n):
    return [name for name, at in SCHEDULE.items() if at[engine] == n]


BX_RING, HC_RING = 8, 4
BX0, HC0, SD0, YG0, ST0 = SLOTS + GP - 1, SLOTS + GP - 1, SLOTS, 2 * DB, 16


def view(t, offset, dims, parts=128, first=0):
    row = t.shape[1]
    return bass.AP(tensor=t, offset=first * row + offset, ap=[[row, parts]] + [list(d) for d in dims])


def prepare(nc, a, w_dram, cat_dram, keep):
    with ExitStack() as ctx:
        sb = lambda name, cols, parts=128: ctx.enter_context(nc.sbuf_tensor(name, [parts, cols], fp32))
        sem = lambda name: ctx.enter_context(nc.semaphore(name))
        ps = ctx.enter_context(nc.psum_tensor("prep_ps", [128, 8 * 512], fp32))
        raw_in = [sb(f"raw_in{m}", 8 * 256) for m in range(2)]
        raw_out = [sb(f"raw_out{m}", 2 * 512) for m in range(2)]
        raw_xp = [sb(f"raw_xp{m}", 512) for m in range(2)]
        raw_dt = [sb(f"raw_dt{m}", DB * DTR) for m in range(2)]
        raw_a = [sb(f"raw_a{m}", DB * NST) for m in range(2)]
        pack = [sb(f"pack{m}", W_COLS) for m in range(2)]
        raw_cat, raw_pg, raw_rec = sb("raw_cat", 2 * 512), sb("raw_pg", 2 * 256), sb("raw_rec", 2 * 128)
        cat_t = sb("cat_t", 4 * 256)
        W2 = CH + 2
        bn = sb("bn", 5 * W2)
        root = sb("root", 2 * W2)
        ident, wpg, wrec, invn, cst = keep["ident"], keep["wpg"], keep["wrec"], keep["invn"], keep["cst"]
        loaded, cleared, placed = sem("prep_loaded"), sem("prep_cleared"), sem("prep_placed")
        turned, copied = sem("prep_turned"), sem("prep_copied")
        a_exp, bn_root, chain, stored = sem("prep_a_exp"), sem("prep_root"), sem("prep_chain"), sem("prep_stored")

        jobs = []
        for m in range(2):
            for k in range(2):
                for h in range(2):
                    src = [raw_in[m][:, (4 * h + r) * 256 + k * 128:(4 * h + r) * 256 + (k + 1) * 128] for r in range(4)]
                    o = W_IN + k * 2 * DIN + h * 512
                    jobs.append((src, 128, 128, pack[m][:, o:o + 512]))
            for jj in range(2):
                src = [raw_out[m][:, fc * 512 + j * 128:fc * 512 + (j + 1) * 128] for j in (2 * jj, 2 * jj + 1) for fc in range(2)]
                jobs.append((src, 128, 128, pack[m][:, W_OUT + jj * 512:W_OUT + (jj + 1) * 512]))
            src = [raw_xp[m][0:XPM, j * 128:(j + 1) * 128] for j in range(DB)]
            jobs.append((src, 128, XPM, pack[m][:, W_XP:W_XP + DB * XPM]))
            src = [raw_dt[m][:, j * DTR:(j + 1) * DTR] for j in range(DB)]
            jobs.append((src, DTR, 128, pack[m][0:DTR, W_DT:W_DT + DIN]))
        for jj in range(2):
            src = [raw_cat[:, oc * 512 + j * 128:oc * 512 + (j + 1) * 128] for j in (2 * jj, 2 * jj + 1) for oc in range(2)]
            jobs.append((src, 128, 128, cat_t[:, jj * 512:(jj + 1) * 512]))
        src = [raw_pg[:, w * 256 + k * 128:w * 256 + (k + 1) * 128] for k in range(2) for w in range(2)]
        jobs.append((src, 128, 128, wpg[:, :]))
        jobs.append(([raw_rec[:, oc * 128:(oc + 1) * 128] for oc in range(2)], 128, 128, wrec[:, :]))

        loads = [(ident[:, :], a["ident"])]
        for m in range(2):
            n = str(m + 1)
            loads.append((raw_in[m][:, :].rearrange("p (r c) -> p r c", r=8), a["L1_conv_in_proj_w" + n].rearrange("(r p) c -> p r c", p=128)))
            loads.append((raw_out[m][:, :].rearrange("p (r c) -> p r c", r=2), a["L1_conv_out_proj_w" + n].rearrange("(r p) c -> p r c", p=128)))
            xp = a["L1_conv_x_proj_w" + n]
            loads.append((raw_xp[m][0:2 * NST, :], xp[DTR:DTR + 2 * NST, :]))
            loads.append((raw_xp[m][2 * NST:XPM, :], xp[0:DTR, :]))
            loads.append((raw_dt[m][:, :].rearrange("p (j c) -> p j c", j=DB), a["L1_conv_dt_proj_w" + n].rearrange("(j p) c -> p j c", p=128)))
            loads.append((raw_a[m][:, :].rearrange("p (j c) -> p j c", j=DB), a["L1_conv_A_log" + n].rearrange("(j p) c -> p j c", p=128)))
        loads.append((raw_cat[:, :].rearrange("p (r c) -> p r c", r=2), a["L1_conv_cat_conv_w"].rearrange("(r p) c -> p r c", p=128)))
        loads.append((raw_pg[:, 0:256], a["L0_conv_w_phi"]))
        loads.append((raw_pg[:, 256:512], a["L0_conv_w_g"]))
        loads.append((raw_rec[:, :].rearrange("p (r c) -> p r c", r=2), a["L0_conv_w_rec"].rearrange("(r p) c -> p r c", p=128)))
        loads.append((keep["wtheta"][:, :], a["L0_conv_w_theta"]))
        loads.append((keep["btheta"][:, :], a["L0_conv_b_theta"].unsqueeze(1)))
        loads.append((keep["pgbias"][:, 0:128], a["L0_conv_b_phi"].partition_broadcast(128)))
        loads.append((keep["pgbias"][:, 128:256], a["L0_conv_b_g"].partition_broadcast(128)))
        loads.append((keep["catb"][:, :], a["L1_conv_cat_conv_b"].rearrange("(o p) -> p o", p=128)))
        for i, n in enumerate(("bn_gamma", "bn_var", "bn_beta", "bn_mean", "b_rec")):
            loads.append((bn[:, i * W2:i * W2 + CH], a["L0_conv_" + n].partition_broadcast(128)))
            loads.append((bn[:, i * W2 + CH:(i + 1) * W2], a["L0_conv_" + n].rearrange("(o p) -> p o", p=128)))
        direct = []
        for m in range(2):
            n = str(m + 1)
            direct.append((pack[m][:, W_CW:W_CW + DB * DCONV].rearrange("p (j c) -> p j c", j=DB), a["L1_conv_conv_w" + n].rearrange("(j p) c -> p j c", p=128)))
            direct.append((pack[m][:, W_CB:W_CB + DB], a["L1_conv_conv_b" + n].rearrange("(j p) -> p j", p=128)))
            direct.append((pack[m][:, W_D:W_D + DB], a["L1_conv_D" + n].rearrange("(j p) -> p j", p=128)))
            direct.append((pack[m][DTR:DTR + 1, W_DT:W_DT + DIN], a["L1_conv_dt_proj_b" + n].unsqueeze(0)))

        with nc.Block() as block, nc.allow_non_contiguous_dma(reason="small per-channel vectors"):
            @block.sync
            def _(sp):
                for dst, src in loads:
                    sp.dma_start(dst, src).then_inc(loaded, 16)
                sp.wait_ge(cleared, 1)
                for dst, src in direct:
                    sp.dma_start(dst, src).then_inc(placed, 16)
                sp.wait_ge(placed, 16 * len(direct))
                sp.wait_ge(copied, len(jobs) + 2)
                for m in range(2):
                    sp.dma_start(w_dram[m], pack[m][:, :]).then_inc(stored, 16)
                sp.dma_start(cat_dram, cat_t[:, :]).then_inc(stored, 16)
                sp.wait_ge(stored, 48)

            @block.scalar
            def _(act):
                act.wait_ge(loaded, 16 * len(loads))
                act.wait_ge(chain, 1)
                nc.scalar.activation(root[:, 0:W2], bn[:, W2:2 * W2], ACT.Sqrt).then_inc(bn_root, 1)
                for m in range(2):
                    nc.scalar.activation(raw_a[m][:, :], raw_a[m][:, :], ACT.Exp).then_inc(a_exp, 1)

            @block.tensor
            def _(pe):
                pe.wait_ge(loaded, 16 * len(loads))
                for i, (srcs, rows, cols, _) in enumerate(jobs):
                    if i >= 4:
                        pe.wait_ge(copied, i - 3)
                    for r, s in enumerate(srcs):
                        o = (i % 4) * 512 + r * cols
                        p = s.shape[0]
                        last = nc.tensor.transpose(ps[0:rows, o:o + cols], s, ident[0:p, 0:p])
                    last.then_inc(turned, 1)

            @block.vector
            def _(dve):
                for m in range(2):
                    last = nc.vector.memset(pack[m][:, W_DT:W_DT + DIN], 0.0)
                last.then_inc(cleared, 1)
                dve.wait_ge(loaded, 16 * len(loads))
                gamma, var, beta, mean, brec = (bn[:, i * W2:(i + 1) * W2] for i in range(5))
                nc.vector.tensor_scalar_add(var, var, BN_EPS).then_inc(chain, 1)
                dve.wait_ge(cleared, 1)
                for i, (srcs, rows, cols, dst) in enumerate(jobs):
                    dve.wait_ge(turned, i + 1)
                    o = (i % 4) * 512
                    nc.vector.tensor_copy(dst, ps[0:rows, o:o + len(srcs) * cols]).then_inc(copied, 1)
                for m in range(2):
                    dve.wait_ge(a_exp, m + 1)
                    nc.vector.tensor_scalar(pack[m][:, W_A:W_A + DB * NST], raw_a[m][:, :], -1.0, A_TOP, ALU.mult, ALU.min).then_inc(copied, 1)
                count = [1]

                def link(ins):
                    count[0] += 1
                    ins.then_inc(chain, 1)
                    dve.wait_ge(chain, count[0])

                r, s = root[:, 0:W2], root[:, W2:2 * W2]
                dve.wait_ge(bn_root, 1)
                link(nc.vector.reciprocal(r, r))
                link(nc.vector.tensor_tensor(s, r, r, ALU.mult))
                link(nc.vector.tensor_tensor(s, s, var, ALU.mult))
                link(nc.vector.tensor_scalar(s, s, -0.5, 1.5, ALU.mult, ALU.add))
                link(nc.vector.tensor_tensor(r, r, s, ALU.mult))
                link(nc.vector.tensor_tensor(r, r, gamma, ALU.mult))
                link(nc.vector.tensor_tensor(s, brec, mean, ALU.subtract))
                link(nc.vector.tensor_tensor(s, s, r, ALU.mult))
                link(nc.vector.tensor_tensor(cst[:, :], s, beta, ALU.add))
                link(nc.vector.tensor_scalar_mul(invn[:, :], r, 1.0 / NPOS))
                link(nc.vector.tensor_tensor(keep["catb"][:, :], keep["catb"][:, :], cst[:, CH:CH + 2], ALU.add))
                link(nc.vector.memset(keep["id2"][:, :], 0.0))
                for k in range(2):
                    link(nc.vector.tensor_copy(keep["id2"][:, k * CH + k * 128:k * CH + (k + 1) * 128], ident[:, :]))
                nc.vector.tensor_copy(keep["btrep"][:, :], keep["btheta"][:, :].to_broadcast([128, 128])).then_inc(chain, 1)


def attention(nc, x_in, u_dram, k_dram, keep):
    PAIRS = 14
    UT = 13
    with ExitStack() as ctx:
        sb = lambda name, cols, parts=128: ctx.enter_context(nc.sbuf_tensor(name, [parts, cols], fp32))
        sem = lambda name: ctx.enter_context(nc.semaphore(name))
        ps = ctx.enter_context(nc.psum_tensor("att_ps", [128, 8 * 512], fp32))
        bank = lambda i: ps[:, i * 512:(i + 1) * 512]
        xb = [sb(f"xb{o}", 2 * NPOS) for o in range(2)]
        ub = [sb(f"ub{o}", 2 * NPOS) for o in range(2)]
        pg = [sb(f"pg{i}", 512) for i in range(2)]
        mt_sb, r_sb = sb("mt_sb", 128), sb("r_sb", CH)
        kn, kp, kb = sb("kn", KCOLS), sb("kp", 2 * CH), sb("kb", CH)
        x_ready = [sem(f"x_ready{o}") for o in range(2)]
        pg_ready, pg_taken, mt_step = sem("pg_ready"), sem("pg_taken"), sem("mt_step")
        k_pe, k_dve, k_stored = sem("k_pe"), sem("k_dve"), sem("k_stored")
        ut_ready, ut_taken = sem("ut_ready"), sem("ut_taken")
        u_stored = [sem(f"u_stored{o}") for o in range(2)]
        wpg, wrec, wtheta = keep["wpg"], keep["wrec"], keep["wtheta"]

        def group(cls, n):
            ks = [cls + 16 * n + 4 * i for i in range(4)]
            return [k for k in ks if k + 1 < NBLK]

        ut_items = [(cls, group(cls, n)) for n in range(3) for cls in (0, 2, 1, 3)] + [("edge", [])]
        assert len(ut_items) == UT

        def token_view(o, k, r, count, parts, first):
            at = []
            for rr in (r, r + 2):
                q = (rr + k) % 4
                if first:
                    q -= 1
                    at.append((q // 2) * NPOS + (NBLK * rr + k - q - 1) // 4)
                else:
                    at.append((q // 2) * NPOS + (NBLK * rr + k - q) // 4)
            return view(ub[o], at[0], [[1, count], [at[1] - at[0], 2], [NBLK, 64]], parts, first)

        with nc.Block() as block:
            @block.sync
            def _(sp):
                sp.sem_inc(ut_ready, 2 * UT)
                with sp.Fori(0, 2) as it:
                    for o in range(2):
                        b = sp.snap(it * 2 + o)
                        sp.wait_ge(ut_ready, it * (2 * UT) + (UT * (o - 1) + 2 * UT))
                        sp.dma_start(xb[o][:, :].rearrange("p (k n) -> p k n", k=2),
                                     x_in[bass.ds(b, 1)].rearrange("b (k p) n -> p (b k) n", p=128)).then_inc(x_ready[o], 16)

            @block.scalar
            def _(act):
                for o in range(2):
                    act.sem_inc(u_stored[o], 16)
                with act.Fori(0, 2) as it:
                    for o in range(2):
                        act.wait_ge(k_dve, it * 8 + (4 * o + 3))
                        act.dma_start(k_dram[bass.ds(it * 2 + o, 1)].rearrange("b p n -> p (b n)"), kn[:, :]).then_inc(k_stored, 16)
                        act.wait_ge(ut_taken, it * (2 * UT) + (UT * (o + 1) + 2))
                        for i in range(TPB):
                            act.dma_start(u_dram[bass.ds((it * 2 + o) * TPB + i, 1)].rearrange("t p (k n) -> p (t k) n", k=2),
                                          ub[o][:, :].rearrange("p (k n) -> p k n", k=2)[:, :, i * T:(i + 1) * T]).then_inc(u_stored[o], 16)
                act.wait_ge(k_stored, 16 * BATCH)
                for o in range(2):
                    act.wait_ge(u_stored[o], 16 + 2 * 16 * TPB)

            @block.tensor
            def _(pe):
                pe.sem_inc(pg_taken, 2)
                pe.sem_inc(ut_taken, 2)
                with pe.Fori(0, 2) as it:
                    for o in range(2):
                        P = lambda c: it * (2 * PAIRS) + (PAIRS * o + c)
                        U = lambda c: it * (2 * UT) + (UT * o + c)

                        def add_pair(i):
                            pe.wait_ge(pg_taken, P(i + 3))
                            for h in range(2):
                                s = pg[i % 2]
                                last = nc.tensor.matmul(bank(2)[:, 0:CMID], s[0:HALF, h * 256 + 128:h * 256 + 256],
                                                        s[0:HALF, h * 256:h * 256 + 128],
                                                        start=(i == 0 and h == 0), stop=(i == PAIRS - 1 and h == 1))
                            last.then_inc(mt_step, 1)

                        pe.wait_ge(x_ready[o], it * 16 + 16)
                        for i in range(PAIRS):
                            pe.wait_ge(pg_taken, P(i + 1))
                            for h in range(2):
                                n0 = (2 * i + h) * HALF
                                for k in range(2):
                                    last = nc.tensor.matmul(bank(i % 2)[0:HALF, h * 256:(h + 1) * 256],
                                                            xb[o][:, k * NPOS + n0:k * NPOS + n0 + HALF],
                                                            wpg[:, k * 256:(k + 1) * 256], start=(k == 0), stop=(k == 1))
                            last.then_inc(pg_ready, 1)
                            if i:
                                add_pair(i - 1)
                        add_pair(PAIRS - 1)
                        pe.wait_ge(k_dve, it * 8 + (4 * o + 1))
                        nc.tensor.matmul(bank(3)[:, 0:CH], mt_sb[:, :], wrec[:, :], start=True, stop=True).then_inc(k_pe, 1)
                        pe.wait_ge(k_dve, it * 8 + (4 * o + 2))
                        for k in range(2):
                            nc.tensor.matmul(bank(4)[:, k * CH:(k + 1) * CH], wtheta[:, k * 128:(k + 1) * 128], r_sb[:, :],
                                             start=True, stop=True)
                        nc.tensor.matmul(bank(5)[:, 0:CH], keep["btrep"][:, :], r_sb[:, :], start=True, stop=True)
                        for k in range(2):
                            last = nc.tensor.matmul(bank(5)[:, CH + k:CH + k + 1], r_sb[:, k * 128:(k + 1) * 128],
                                                    keep["btheta"][:, :], start=True, stop=True)
                        last.then_inc(k_pe, 1)
                        pe.wait_ge(k_dve, it * 8 + (4 * o + 4))
                        for i, (cls, ks) in enumerate(ut_items):
                            pe.wait_ge(ut_taken, U(i + 1))
                            b = bank(6 + (i + o) % 2)
                            if cls == "edge":
                                for rows, n0, par in ((0, 64 * (NBLK - 1), 0), (64, 0, 1)):
                                    for k2 in range(2):
                                        last = nc.tensor.matmul(b[rows:rows + 64, rows * 2:rows * 2 + 128],
                                                                xb[o][:, k2 * NPOS + n0:k2 * NPOS + n0 + 64],
                                                                kp[:, k2 * CH + par * 128:k2 * CH + par * 128 + 128],
                                                                start=(k2 == 0), stop=(k2 == 1))
                            for j, kk in enumerate(ks):
                                par = kk % 2
                                for k2 in range(2):
                                    n0 = k2 * NPOS + 64 * kk
                                    last = nc.tensor.matmul(b[:, j * 128:(j + 1) * 128], xb[o][:, n0:n0 + 128],
                                                            kp[:, k2 * CH + par * 128:k2 * CH + par * 128 + 128],
                                                            start=(k2 == 0), stop=(k2 == 1))
                            last.then_inc(ut_ready, 1)

            @block.vector
            def _(dve):
                dve.sem_inc(mt_step, 2)
                with dve.Fori(0, 2) as it:
                    for o in range(2):
                        P = lambda c: it * (2 * PAIRS) + (PAIRS * o + c)
                        K = lambda c: it * 8 + (4 * o + c)
                        for i in range(PAIRS):
                            dve.wait_ge(pg_ready, P(i + 1))
                            dve.wait_ge(mt_step, P(i + 1))
                            nc.vector.tensor_tensor(view(pg[i % 2], 0, [[256, 2], [1, 256]], HALF),
                                                    bank(i % 2)[0:HALF, :].rearrange("p (h c) -> p h c", h=2),
                                                    view(keep["pgbias"], 0, [[0, 2], [1, 256]], HALF), ALU.add).then_inc(pg_taken, 1)
                        dve.wait_ge(mt_step, P(PAIRS + 2))
                        nc.vector.tensor_copy(mt_sb[:, :], bank(2)[:, 0:CMID]).then_inc(k_dve, 1)
                        dve.wait_ge(k_pe, it * 4 + (2 * o + 1))
                        nc.vector.tensor_tensor(r_sb[:, :], bank(3)[:, 0:CH], keep["invn"][:, 0:CH], ALU.mult).then_inc(k_dve, 1)
                        dve.wait_ge(k_pe, it * 4 + (2 * o + 2))
                        if o == 0:
                            dve.wait_ge(keep["kn_free"], it * 1 + 1)
                        else:
                            dve.wait_ge(k_stored, it * 32 + 16)
                        nc.vector.tensor_tensor(kn[:, 0:2 * CH], bank(4), keep["id2"][:, :], ALU.add)
                        order = [[64, 2], [128, 2], [1, 64]]
                        nc.vector.tensor_tensor(view(kb, 0, order), view(ps, 5 * 512, [[2, 2], [1, 2], [4, 64]]),
                                                view(keep["cst"], 0, [[2, 2], [1, 2], [4, 64]]), ALU.add)
                        nc.vector.tensor_tensor(kn[:, 2 * CH:2 * CH + 2], bank(5)[:, CH:CH + 2], keep["catb"][:, :], ALU.add).then_inc(k_dve, 1)
                        dve.wait_ge(k_dve, K(3))
                        for k in range(2):
                            last = nc.vector.tensor_copy(view(kp, k * CH, order), view(kn, k * CH, [[2, 2], [1, 2], [4, 64]]))
                        last.then_inc(k_dve, 1)
                        dve.wait_ge(u_stored[o], it * (16 * TPB) + 16)
                        for i, (cls, ks) in enumerate(ut_items):
                            dve.wait_ge(ut_ready, it * (2 * UT) + (UT * o + i + 1 + 2 * UT))
                            if i == 0:
                                dve.wait_ge(k_dve, K(4))
                            b = (6 + (i + o) % 2) * 512
                            if cls == "edge":
                                nc.vector.tensor_tensor(token_view(o, NBLK - 1, 0, 1, 64, 0), view(ps, b, [[128, 1], [64, 2], [1, 64]], 64),
                                                        view(kb, 0, [[0, 1], [64, 2], [1, 64]], 64), ALU.add)
                                nc.vector.tensor_tensor(token_view(o, 0, 1, 1, 64, 64), view(ps, b + 128, [[128, 1], [64, 2], [1, 64]], 64, 64),
                                                        view(kb, 128, [[0, 1], [64, 2], [1, 64]], 64, 64), ALU.add).then_inc(ut_taken, 1)
                            else:
                                par = cls % 2
                                nc.vector.tensor_tensor(token_view(o, ks[0], par, len(ks), 128, 0),
                                                        view(ps, b, [[128, len(ks)], [64, 2], [1, 64]]),
                                                        view(kb, par * 128, [[0, len(ks)], [64, 2], [1, 64]]), ALU.add).then_inc(ut_taken, 1)

            @block.gpsimd
            def _(pool):
                pool.sem_inc(keep["kn_free"], 1)
                pool.wait_ge(k_stored, 32)
                pool.sem_inc(keep["kn_free"], 1)


def mambas(nc, u_dram, w_dram, y_dram, bc_dram, keep):
    with ExitStack() as ctx:
        sb = lambda name, cols, parts=128, dt=fp32: ctx.enter_context(nc.sbuf_tensor(name, [parts, cols], dt))
        sem = lambda name: ctx.enter_context(nc.semaphore(name))
        ps = ctx.enter_context(nc.psum_tensor("mamba_ps", [128, 8 * 512], fp32))
        bank = lambda i: ps[:, i * 512:(i + 1) * 512]
        decay = [ps[:, i * 1024:i * 1024 + 2 * T] for i in range(2)]
        y_ps = [bank(4)[:, 0:T], bank(5)[:, 0:T]]
        work = [bank(6), bank(7)]

        w = sb("w", W_COLS)
        u = [sb(f"u{p}", 2 * T) for p in range(2)]
        x = [sb(f"x{p}", DB * T) for p in range(2)]
        sz = [sb(f"sz{p}", DB * T) for p in range(2)]
        dt = [sb(f"dt{p}", DB * T) for p in range(2)]
        dtx = [sb(f"dtx{p}", DB * T) for p in range(2)]
        b_all, c_all = sb("b_all", NST * T), sb("c_all", NST * T)
        dbx = [sb(f"dbx{i}", 2 * T) for i in range(BX_RING)]
        hc = [sb(f"hc{i}", 2 * T) for i in range(HC_RING)]
        skip = sb("skip", DB * 128)
        yg = sb("yg", DB * T)
        ytok = sb("ytok", 4 * FEAT, TCH)
        bc_rows = sb("bc_rows", T, 2 * NST)
        dtr = sb("dtr", T, 32)
        soft, neg_ln_one = sb("soft", DB * T), sb("neg_ln_one", 1)
        restart = sb("restart", 4 * TSEQ)
        ident = keep["ident"]

        w_ready, y_stored, u_wrapped = sem("w_ready"), sem("y_stored"), sem("u_wrapped")
        u_ready = [sem(f"u_ready{p}") for p in range(2)]
        work_ready, work_free = sem("work_ready"), [sem(f"work_free{p}") for p in range(2)]
        acc_ready, conv_chain = sem("acc_ready"), sem("conv_chain")
        silu_ready = sem("silu_ready")
        rows_ready, rows_stored = sem("rows_ready"), sem("rows_stored")
        b_loaded, c_loaded = ([sem(f"{n}_loaded{g}") for g in range(GP)] for n in "bc")
        abs_ready, exp_ready, one_plus_ready = sem("abs_ready"), sem("exp_ready"), sem("one_plus_ready")
        lost_ready, ln_ready, dtx_ready = sem("lost_ready"), sem("ln_ready"), sem("dtx_ready")
        decay_ready, dbx_ready = sem("decay_ready"), sem("dbx_ready")
        scan_done, hc_ready, sums_done = sem("scan_done"), sem("hc_ready"), sem("sums_done")
        skip_ready, yg_ready, ones_set, restart_set = sem("skip_ready"), sem("yg_ready"), sem("ones_set"), sem("restart_set")
        ln_one_ready, ln_chain = sem("ln_one_ready"), sem("ln_chain")

        win = lambda k, c0: w[:, W_IN + k * 2 * DIN + c0:W_IN + k * 2 * DIN + c0 + 128]
        blk = lambda t, j: t[:, j * T:(j + 1) * T]
        pair = lambda t, h: t[:, 2 * h * T:(2 * h + 2) * T]
        seqs = lambda ap: ap.rearrange("p (s t) -> p s t", t=SEQ)

        class Step:

            def __init__(self, q, o, first=False, last=False):
                self.q, self.o, self.first, self.last = q, o, first, last
                self.par = o % 2

            def at(self, per_step, c):
                return self.q * (2 * per_step) + (per_step * self.o + c)

            def item(self, name):
                if name.startswith("end"):
                    return Item(self.q, ITEMS * self.o + ITEMS - 4 + len(OUTS) + int(name[-1]))
                order = list(SCHEDULE) if not self.last else OUTS
                return Item(self.q, ITEMS * self.o + ITEMS - 4 + order.index(name))

            def front(self):
                return Front(self.q, self.o + 1, ITEMS * self.o + ITEMS - 4 + (len(OUTS) if self.first else 0),
                             FRONT if self.first else list(SCHEDULE))

        class Item:

            def __init__(self, q, c):
                self.q, self.c, self.slot = q, c, c % 2

            def ready(self):
                return self.q * (2 * ITEMS) + (self.c + 1)

            def freed(self):
                return self.q * ITEMS + (self.c // 2 + 2)

            def bank_is_free(self):
                return self.q * ITEMS + (self.c // 2 + 1)

        class Front:

            def __init__(self, q, o, base, order):
                self.q, self.o, self.par, self.base, self.order = q, o, o % 2, base, order

            def at(self, per_step, c):
                return self.q * (2 * per_step) + (per_step * self.o + c)

            def item(self, name):
                return Item(self.q, self.base + self.order.index(name))

            def u_wait(self):
                return self.q * 16 + (self.o // 2 + 1) * 16

        def program(eng, front_prologue, step, before_pass=None, after_pass=None):
            with eng.Fori(0, 2) as m:
                q0 = m * (TILES // 2)
                if before_pass:
                    before_pass(m)
                front_prologue(Front(q0, 0, 0, FRONT))
                step(Step(q0, 0, first=True), 0)
                with eng.Fori(0, TILES // 2 - 1) as i:
                    q = m * (TILES // 2) + i
                    step(Step(q, 1), i)
                    step(Step(q, 2), i)
                step(Step(m * (TILES // 2) + (TILES // 2 - 1), 1, last=True), TILES // 2 - 1)

        with nc.Block() as block:
            @block.sync
            def _(sp):
                sp.dma_start(u_dram[TILES], u_dram[0]).then_inc(u_wrapped, 16)
                sp.wait_ge(u_wrapped, 16)

                def load_u(par, tile):
                    sp.dma_start(u[par][:, :], u_dram[bass.ds(tile, 1)].rearrange("t p n -> p (t n)")).then_inc(u_ready[par], 16)

                def before(m):
                    sp.wait_ge(y_stored, m * (16 * TILES) + ST0)
                    sp.dma_start(w[:, :], w_dram[bass.ds(m, 1)].rearrange("m p n -> p (m n)")).then_inc(w_ready, 16)

                def spread_bc(f):
                    sp.wait_ge(rows_ready, f.at(1, 1))
                    for r in (0, NST):
                        sp.dma_start(bc_dram[f.par, r:r + NST], bc_rows[r:r + NST, :]).then_inc(rows_stored, 16)
                    sp.wait_ge(rows_stored, f.at(32, 32))
                    flat = bc_dram[f.par].rearrange("r t -> (r t)")
                    for g in range(GP):
                        for dst, r, used, credit, arrived in ((b_all, 0, dbx_ready, BX0, b_loaded), (c_all, NST, hc_ready, HC0, c_loaded)):
                            sp.wait_ge(used, f.at(SLOTS, g + 1 - GP + credit))
                            src = flat[(r + 2 * g) * T:(r + 2 * g + 2) * T].partition_broadcast(128)
                            sp.dma_start(dst[:, 2 * g * T:(2 * g + 2) * T], src).then_inc(arrived[g], 16)

                def front(f):
                    spread_bc(f)

                def store(s, n):
                    tile = sp.snap(s.at(1, n - 1))
                    it = s.item("out1") if n == 0 else s.item("end1")
                    sp.wait_ge(work_free[it.slot], it.freed())
                    sp.dma_start(y_dram[bass.ds(tile, 1)].rearrange("t (c p) f -> p (t c) f", p=TCH),
                                 ytok[:, :].rearrange("p (c f) -> p c f", f=FEAT)).then_inc(y_stored, 16)

                def step(s, i):
                    sp.wait_ge(work_ready, s.at(ITEMS, ITEMS - 2 if s.first else ITEMS - 4))
                    tile = 1 if s.last else (2 if s.first else sp.snap(i * 2 + (s.o + 2)))
                    load_u(s.par, tile)
                    if not s.first:
                        store(s, 0)
                    if s.last:
                        store(s, 1)
                    else:
                        spread_bc(s.front())

                sp.sem_inc(y_stored, ST0)
                for p in range(2):
                    load_u(p, p)
                program(sp, front, step, before)
                sp.wait_ge(y_stored, 2 * 16 * TILES + ST0)
                for p in range(2):
                    sp.wait_ge(u_ready[p], 16 * (TILES + 1))

            @block.tensor
            def _(pe):
                def take(item):
                    pe.wait_ge(work_free[item.slot], item.bank_is_free())
                    return work[item.slot]

                def in_proj(f, item, c0):
                    b = take(item)
                    for k in range(2):
                        last = nc.tensor.matmul(b[:, 0:T], win(k, c0), u[f.par][:, k * T:(k + 1) * T], start=(k == 0), stop=(k == 1))
                    last.then_inc(work_ready, 1)

                def x_proj(f):
                    pe.wait_ge(silu_ready, f.at(2, 1))
                    b = take(f.item("xp"))
                    for j in range(DB):
                        last = nc.tensor.matmul(b[0:XPM, 0:T], w[:, W_XP + j * XPM:W_XP + (j + 1) * XPM], blk(x[f.par], j),
                                                start=(j == 0), stop=(j == DB - 1))
                    last.then_inc(work_ready, 1)

                def dt_proj(f, j):
                    b = take(f.item(f"dt{j}"))
                    nc.tensor.matmul(b[:, 0:T], w[0:DTR + 1, W_DT + j * 128:W_DT + (j + 1) * 128], dtr[0:DTR + 1, :],
                                     start=True, stop=True).then_inc(work_ready, 1)

                def out_proj(item, c):
                    h = c % 2
                    b = take(item) if h == 0 else work[item.slot]
                    for j in range(DB):
                        last = nc.tensor.matmul(b[0:TCH, h * FEAT:(h + 1) * FEAT],
                                                yg[:, j * T + c * TCH:j * T + (c + 1) * TCH],
                                                w[:, W_OUT + j * FEAT:W_OUT + (j + 1) * FEAT], start=(j == 0), stop=(j == DB - 1))
                    if h == 1:
                        last.then_inc(work_ready, 1)

                def sums(s, n):
                    j, g = n // GP, n % GP
                    if g == 0:
                        pe.wait_ge(yg_ready, s.at(DB, j - 1 + YG0))
                        nc.tensor.matmul(y_ps[j % 2], skip[:, j * 128:(j + 1) * 128], blk(x[s.par], j), start=True, stop=False)
                    pe.wait_ge(hc_ready, s.at(SLOTS, n + 1 + HC0))
                    for e in range(2):
                        last = nc.tensor.matmul(y_ps[j % 2], ident[:, :], hc[g % HC_RING][:, e * T:(e + 1) * T],
                                                start=False, stop=(g == GP - 1 and e == 1))
                    last.then_inc(sums_done, 1)

                def front_slot(f, n):
                    for name in due(0, n):
                        if name == "x0":
                            pe.wait_ge(u_ready[f.par], f.u_wait())
                        if name[0] == "x" and name != "xp":
                            in_proj(f, f.item(name), int(name[1]) * 128)
                        if name[0] == "z":
                            in_proj(f, f.item(name), DIN + int(name[1]) * 128)
                        if name == "xp":
                            x_proj(f)
                        if name == "dt0":
                            it = f.item("xp")
                            pe.wait_ge(work_free[it.slot], it.freed())
                        if name[:2] == "dt":
                            dt_proj(f, int(name[2]))

                def before(m):
                    pe.wait_ge(w_ready, m * 16 + 16)
                    pe.wait_ge(skip_ready, m * DB + DB)

                def front(f):
                    for n in range(SLOTS):
                        front_slot(f, n)

                def step(s, i):
                    for n in range(SLOTS):
                        for half in range(2):
                            for name in due(0, n - half):
                                if name in OUTS and not s.first:
                                    i = int(name[-1])
                                    if i == 0 and half == 0:
                                        pe.wait_ge(yg_ready, s.at(DB, YG0))
                                    out_proj(s.item(name), 2 * i + half)
                        if not s.last:
                            front_slot(s.front(), n)
                        if n > 0:
                            sums(s, n - 1)
                    sums(s, SLOTS - 1)
                    if s.last:
                        pe.wait_ge(yg_ready, s.at(DB, DB + YG0))
                        for c in range(4):
                            out_proj(s.item(f"end{c // 2}"), c)

                for p in range(2):
                    pe.sem_inc(work_free[p], 1)
                program(pe, front, step, before)

            @block.scalar
            def _(act):
                def take(item):
                    act.wait_ge(work_ready, item.ready())
                    return work[item.slot]

                def decays(s, n):
                    j, g = n // GP, n % GP
                    if g == 0 and j % 2 == 0:
                        act.wait_ge(dtx_ready, s.at(8, 4 * (j // 2) + 4))
                    act.wait_ge(hc_ready, s.at(SLOTS, n + 1 + HC0 - 2))
                    for e in range(2):
                        c = W_A + j * NST + 2 * g + e
                        last = nc.scalar.activation(decay[g % 2][:, e * T:(e + 1) * T], blk(dt[s.par], j), ACT.Exp, scale=w[:, c:c + 1])
                    last.then_inc(decay_ready, 1)

                def front_slot(f, n, wait_x=True):
                    for name in due(1, n):
                        if name in OUTS:
                            continue
                        it, j = f.item(name), int(name[-1]) if name != "xp" else 0
                        if name[0] == "x" and name != "xp":
                            if j == 0 and wait_x:
                                act.wait_ge(sums_done, f.at(SLOTS, SLOTS - GP + 1 - 2 * SLOTS + SD0))
                            nc.scalar.activation(blk(x[f.par], j), take(it)[:, 0:T], ACT.Identity,
                                                 scale=w[:, W_CW + j * DCONV + DCONV - 1:W_CW + (j + 1) * DCONV],
                                                 bias=w[:, W_CB + j:W_CB + j + 1]).then_inc(acc_ready, 1)
                        if name[0] == "z":
                            if j == 0:
                                act.wait_ge(yg_ready, f.at(DB, YG0 - DB))
                            nc.scalar.copy(blk(sz[f.par], j), take(it)[:, 0:T]).then_inc(work_free[it.slot], 1)
                        if name == "xp":
                            b = take(it)
                            nc.scalar.copy(bc_rows[:, :], b[0:2 * NST, 0:T]).then_inc(rows_ready, 1)
                            nc.scalar.copy(dtr[0:DTR, :], b[2 * NST:XPM, 0:T]).then_inc(work_free[it.slot], 1)
                        if name[:2] == "dt":
                            h = j // 2
                            v = take(it)[:, 0:T]
                            nc.scalar.activation(blk(dtx[f.par], j), v, ACT.Abs).then_inc(abs_ready, 1)
                            nc.scalar.activation(blk(dt[f.par], j), v, ACT.Relu).then_inc(work_free[it.slot], 1)
                            if j % 2 == 1:
                                e = pair(dtx[f.par], h)
                                act.wait_ge(abs_ready, f.at(DB, j + 1))
                                nc.scalar.activation(e, e, ACT.Exp, scale=-1.0).then_inc(exp_ready, 1)
                                act.wait_ge(exp_ready, f.at(2, h + 1))
                                nc.scalar.activation(pair(soft, h), e, ACT.Identity, bias=1.0).then_inc(one_plus_ready, 1)
                    if n == SILU_X_AT:
                        it = f.item("x3")
                        act.wait_ge(work_free[it.slot], it.freed())
                        nc.scalar.activation(x[f.par][:, :], x[f.par][:, :], ACT.Silu).then_inc(silu_ready, 1)
                        nc.scalar.preload_act_table_set(EXP_SET)
                    if n == LN_AT:
                        act.wait_ge(lost_ready, f.at(2, 2))
                        nc.scalar.activation(soft[:, :], soft[:, :], ACT.Ln).then_inc(ln_chain, 1)
                        nc.scalar.preload_act_table_set(EXP_SET)
                    if n == LN_LESS_AT:
                        act.wait_ge(ln_chain, f.at(1, 2))
                        nc.scalar.activation(soft[:, :], soft[:, :], ACT.Identity, bias=neg_ln_one[:, 0:1]).then_inc(ln_ready, 1)
                    if n == SILU_Z_AT:
                        it = f.item("z3")
                        act.wait_ge(work_free[it.slot], it.freed())
                        nc.scalar.activation(sz[f.par][:, :], sz[f.par][:, :], ACT.Silu).then_inc(silu_ready, 1)
                        nc.scalar.preload_act_table_set(EXP_SET)

                def before(m):
                    act.wait_ge(w_ready, m * 16 + 16)

                def front(f):
                    for n in range(SLOTS):
                        front_slot(f, n, wait_x=False)

                def step(s, i):
                    for n in range(SLOTS):
                        decays(s, n)
                        for name in due(1, n):
                            if name in OUTS and not s.first:
                                out_copy(s, 0, int(name[-1]), s.item(name))
                        if not s.last:
                            front_slot(s.front(), n)
                    if s.last:
                        for i in range(2):
                            out_copy(s, 1, i, s.item(f"end{i}"))

                def out_copy(s, n, i, item):
                    if i == 0:
                        act.wait_ge(y_stored, s.at(16, 16 * (n - 1) + ST0))
                    nc.scalar.copy(ytok[:, i * 512:(i + 1) * 512], take(item)[0:TCH, :]).then_inc(work_free[item.slot], 1)

                act.wait_ge(ones_set, 1)
                act.wait_ge(ones_set, 2)
                nc.scalar.activation(neg_ln_one[:, :], neg_ln_one[:, :], ACT.Ln).then_inc(ln_chain, 1)
                act.wait_ge(ln_chain, 1)
                nc.scalar.activation(neg_ln_one[:, :], neg_ln_one[:, :], ACT.Identity, scale=-1.0).then_inc(ln_one_ready, 1)
                act.wait_ge(ln_one_ready, 1)
                nc.scalar.preload_act_table_set(EXP_SET)
                program(act, front, step, before)

            @block.vector
            def _(dve):
                def conv(f, j):
                    it = f.item(f"x{j}")
                    dve.wait_ge(acc_ready, f.at(DB, j + 1))
                    for back in range(1, DCONV):
                        c = W_CW + j * DCONV + DCONV - 1 - back
                        dst = seqs(blk(x[f.par], j))[:, :, back:SEQ]
                        src = seqs(work[it.slot][:, 0:T])[:, :, 0:SEQ - back]
                        last = nc.vector.scalar_tensor_tensor(dst, src, w[:, c:c + 1], dst, ALU.mult, ALU.add)
                        if back < DCONV - 1:
                            last.then_inc(conv_chain, 1)
                            dve.wait_ge(conv_chain, f.at(2 * DB, 2 * j + back))
                    last.then_inc(work_free[it.slot], 1)

                def front_slot(f, n):
                    for name in due(2, n):
                        if name[0] == "x":
                            conv(f, int(name[1]))
                        if name[:2] == "dt":
                            h = int(name[2]) // 2
                            e = pair(dtx[f.par], h)
                            dve.wait_ge(one_plus_ready, f.at(2, h + 1))
                            nc.vector.scalar_tensor_tensor(e, pair(soft, h), 1.0, e, ALU.subtract, ALU.subtract).then_inc(lost_ready, 1)

                def gate(s, j, par, sums):
                    dve.wait_ge(sums_done, sums)
                    nc.vector.tensor_tensor(blk(yg, j), y_ps[j % 2], blk(sz[par], j), ALU.mult).then_inc(yg_ready, 1)

                def recur(s, n):
                    j, g = n // GP, n % GP
                    h = decay[g % 2]
                    dve.wait_ge(decay_ready, s.at(SLOTS, n + 1))
                    dve.wait_ge(dbx_ready, s.at(SLOTS, n + 1 + BX0))
                    nc.vector.tensor_tensor_scan(h, h, dbx[g % BX_RING][:, :], 0.0, ALU.mult, ALU.add).then_inc(scan_done, 1)
                    if j == 0:
                        dve.wait_ge(c_loaded[g], s.at(16, 16))
                    dve.wait_ge(sums_done, s.at(SLOTS, n + 1 - HC_RING + SD0))
                    dve.wait_ge(scan_done, s.at(SLOTS, n + 1 + BX_RING))
                    nc.vector.tensor_tensor(hc[g % HC_RING][:, :], h, c_all[:, 2 * g * T:(2 * g + 2) * T], ALU.mult).then_inc(hc_ready, 1)

                def front(f):
                    for n in range(SLOTS):
                        front_slot(f, n)

                def before(m):
                    dve.wait_ge(w_ready, m * 16 + 16)
                    for j in range(DB):
                        nc.vector.tensor_scalar_mul(skip[:, j * 128:(j + 1) * 128], ident[:, :], w[:, W_D + j:W_D + j + 1]).then_inc(skip_ready, 1)

                def step(s, i):
                    for n in range(SLOTS):
                        recur(s, n)
                        if n == 2 and not s.first:
                            gate(s, DB - 1, 1 - s.par, s.at(SLOTS, SD0))
                        if n in GATE_AT:
                            j = GATE_AT.index(n)
                            if j == 0:
                                dve.wait_ge(silu_ready, s.at(2, 2))
                            if j == 0 and not s.first:
                                dve.wait_ge(work_ready, s.item("out1").ready())
                            gate(s, j, s.par, s.at(SLOTS, GP * (j + 1) + SD0))
                        if not s.last:
                            front_slot(s.front(), n)
                    if s.last:
                        gate(s, DB - 1, s.par, s.at(SLOTS, SLOTS + SD0))

                nc.vector.memset(dtr[:, :], 1.0).then_inc(ones_set, 1)
                nc.vector.memset(neg_ln_one[:, :], 1.0).then_inc(ones_set, 1)
                dve.sem_inc(sums_done, SD0)
                dve.sem_inc(hc_ready, HC0)
                dve.sem_inc(yg_ready, YG0)
                program(dve, front, step, before)

            @block.gpsimd
            def _(pool):
                def make_dtx(f, k):
                    h, part = k // 4, k % 4
                    d, dx = pair(dt[f.par], h), pair(dtx[f.par], h)
                    if part == 0:
                        pool.wait_ge(ln_ready, f.at(1, 1))
                        ins = nc.gpsimd.tensor_tensor(d, d, pair(soft, h), ALU.add)
                    else:
                        pool.wait_ge(dtx_ready, f.at(8, k))
                        if part == 1:
                            ins = nc.gpsimd.tensor_tensor(d, d, dx, ALU.subtract)
                        elif part == 2:
                            ins = nc.gpsimd.tensor_tensor(dx, d, pair(x[f.par], h), ALU.mult)
                        else:
                            ins = nc.gpsimd.tensor_tensor(seqs(d)[:, :, 0], restart[:, 0:2 * TSEQ], restart[:, 2 * TSEQ:4 * TSEQ], ALU.mult)
                    ins.then_inc(dtx_ready, 1)

                def make_dbx(s, n):
                    j, g = n // GP, n % GP
                    if g == 0 and j % 2 == 0:
                        pool.wait_ge(dtx_ready, s.at(8, 4 * (j // 2) + 4))
                    if j == 0:
                        pool.wait_ge(b_loaded[g], s.at(16, 16))
                    pool.wait_ge(scan_done, s.at(SLOTS, n + 1))
                    nc.gpsimd.tensor_tensor(view(dbx[g % BX_RING], 0, [[T, 2], [1, T]]), view(dtx[s.par], j * T, [[0, 2], [1, T]]),
                                            view(b_all, 2 * g * T, [[T, 2], [1, T]]), ALU.mult).then_inc(dbx_ready, 1)

                def front(f):
                    for k in range(4):
                        make_dtx(f, k)

                def step(s, i):
                    for n in range(SLOTS):
                        make_dbx(s, n)
                        if n in DTX_LATE:
                            make_dtx(s, 4 + DTX_LATE.index(n))
                        if not s.last and n in DTX_EARLY:
                            make_dtx(s.front(), DTX_EARLY.index(n))

                nc.gpsimd.memset(restart[:, 0:2 * TSEQ], RESTART)
                nc.gpsimd.memset(restart[:, 2 * TSEQ:4 * TSEQ], 1.0).then_inc(restart_set, 1)
                pool.wait_ge(restart_set, 1)
                pool.sem_inc(dbx_ready, BX0)
                pool.sem_inc(scan_done, BX_RING)
                program(pool, front, step)


def finish(nc, x_in, y_dram, k_dram, cat_dram, out, keep):
    with ExitStack() as ctx:
        sb = lambda name, cols: ctx.enter_context(nc.sbuf_tensor(name, [128, cols], fp32))
        sem = lambda name: ctx.enter_context(nc.semaphore(name))
        ps = ctx.enter_context(nc.psum_tensor("fin_ps", [128, 8 * 512], fp32))
        src = [sb(f"src{i}", 6 * T) for i in range(TPB)]
        res = [sb(f"res{i}", 2 * T) for i in range(TPB)]
        cat_t, maps, now = sb("cat_tt", 4 * CH), sb("maps", BATCH * KCOLS), sb("now", KCOLS)
        fixed, src_ready = sem("fixed"), [sem(f"src_ready{i}") for i in range(TPB)]
        now_ready, made, taken = sem("now_ready"), sem("made"), sem("taken")
        stored = [sem(f"out_stored{i}") for i in range(TPB)]
        y_img = y_dram.rearrange("(m b t) n f -> m b (t n f)", m=2, b=BATCH).rearrange("m b (k p n) -> m b p k n", k=2, p=128)

        with nc.Block() as block:
            @block.sync
            def _(sp):
                sp.dma_start(cat_t[:, :], cat_dram).then_inc(fixed, 16)
                sp.dma_start(maps[:, :].rearrange("p (b n) -> p b n", b=BATCH), k_dram.rearrange("b p n -> p b n")).then_inc(fixed, 16)
                sp.sem_inc(made, TPB)
                with sp.Fori(0, BATCH) as b:
                    for i in range(TPB):
                        sp.wait_ge(made, b * TPB + (i + 1))
                        s = src[i][:, :].rearrange("p (k n) -> p k n", k=6)
                        for m in range(2):
                            sp.dma_start(s[:, 2 * m:2 * m + 2, :], y_img[m][bass.ds(b, 1)].rearrange("b p k n -> p (b k) n")[:, :, i * T:(i + 1) * T]).then_inc(src_ready[i], 16)
                        sp.dma_start(s[:, 4:6, :], x_in[bass.ds(b, 1)].rearrange("b (k p) n -> p (b k) n", p=128)[:, :, i * T:(i + 1) * T]).then_inc(src_ready[i], 16)

            @block.vector
            def _(dve):
                dve.sem_inc(taken, TPB)
                dve.wait_ge(fixed, 32)
                with dve.Fori(0, BATCH) as b:
                    dve.wait_ge(made, b * TPB + TPB)
                    dve.wait_ge(taken, b * TPB + TPB)
                    nc.vector.tensor_copy(now[:, :], maps[:, bass.ds(b * KCOLS, KCOLS)]).then_inc(now_ready, 1)

            @block.tensor
            def _(pe):
                pe.wait_ge(fixed, 32)
                with pe.Fori(0, BATCH) as b:
                    pe.wait_ge(now_ready, b + 1)
                    for i in range(TPB):
                        pe.wait_ge(src_ready[i], b * 48 + 48)
                        back = 4 if i >= 4 else (7 if i == 3 else 3)
                        pe.wait_ge(taken, b * TPB + (i + 1 - back + TPB))
                        for oc in range(2):
                            o = ((i % 4) * 2 + oc) * 512
                            for k in range(6):
                                w = cat_t[:, k * CH + oc * 128:k * CH + (oc + 1) * 128] if k < 4 else \
                                    now[:, (k - 4) * CH + oc * 128:(k - 4) * CH + (oc + 1) * 128]
                                last = nc.tensor.matmul(ps[:, o:o + T], w, src[i][:, k * T:(k + 1) * T], start=(k == 0), stop=(k == 5))
                        last.then_inc(made, 1)

            @block.scalar
            def _(act):
                for i in range(TPB):
                    act.sem_inc(stored[i], 16)
                with act.Fori(0, BATCH) as b:
                    for i in range(TPB):
                        act.wait_ge(made, b * TPB + (i + 1 + TPB))
                        act.wait_ge(stored[i], b * 16 + 16)
                        for oc in range(2):
                            o = ((i % 4) * 2 + oc) * 512
                            last = nc.scalar.activation(res[i][:, oc * T:(oc + 1) * T], ps[:, o:o + T], ACT.Identity,
                                                        bias=now[:, 2 * CH + oc:2 * CH + oc + 1])
                        last.then_inc(taken, 1)
                        act.wait_ge(taken, b * TPB + (i + 1 + TPB))
                        act.dma_start(out[bass.ds(b, 1)].rearrange("b (k p) n -> p (b k) n", p=128)[:, :, i * T:(i + 1) * T],
                                      res[i][:, :].rearrange("p (k n) -> p k n", k=2)).then_inc(stored[i], 16)
                for i in range(TPB):
                    act.wait_ge(stored[i], 16 * BATCH + 16)


def build(nc, a, out):
    x_in = a["x"].rearrange("b c h w -> b c (h w)")
    out = out.rearrange("b c h w -> b c (h w)")
    w_dram = nc.dram_tensor("w_scratch", [2, 128, W_COLS], fp32).ap()
    cat_dram = nc.dram_tensor("cat_scratch", [128, 4 * CH], fp32).ap()
    u_dram = nc.dram_tensor("u_scratch", [TILES + 1, 128, 2 * T], fp32).ap()
    k_dram = nc.dram_tensor("k_scratch", [BATCH, 128, KCOLS], fp32).ap()
    y_dram = nc.dram_tensor("y_scratch", [2 * TILES, T, FEAT], fp32).ap()
    bc_dram = nc.dram_tensor("bc_scratch", [2, 2 * NST, T], fp32).ap()
    with ExitStack() as ctx:
        keep = {"ident": ctx.enter_context(nc.sbuf_tensor("ident", [128, 128], fp32))}
        keep["kn_free"] = ctx.enter_context(nc.semaphore("kn_free"))
        with ExitStack() as early:
            for name, cols in (("wpg", 512), ("wrec", 256), ("wtheta", 256), ("btheta", 1), ("btrep", 128), ("pgbias", 256),
                               ("invn", CH + 2), ("cst", CH + 2), ("catb", 2), ("id2", 2 * CH)):
                keep[name] = early.enter_context(nc.sbuf_tensor(name, [128, cols], fp32))
            prepare(nc, a, w_dram, cat_dram, keep)
            attention(nc, x_in, u_dram, k_dram, keep)
        mambas(nc, u_dram, w_dram, y_dram, bc_dram, keep)
        finish(nc, x_in, y_dram, k_dram, cat_dram, out, keep)


_INS = ["x"] + ["L0_conv_" + n for n in ("w_theta", "b_theta", "w_phi", "b_phi", "w_g", "b_g", "w_rec", "b_rec", "bn_gamma",
                                         "bn_beta", "bn_mean", "bn_var")] + \
       ["L1_conv_" + n + m for m in "12" for n in ("in_proj_w", "conv_w", "conv_b", "x_proj_w", "dt_proj_w", "dt_proj_b",
                                                   "A_log", "D", "out_proj_w")] + ["L1_conv_cat_conv_w", "L1_conv_cat_conv_b"]


def kernel(**inputs):
    import numpy as np
    import concourse.bacc as bacc
    from concourse.bass_utils import run_bass_kernel_spmd

    nc = bacc.Bacc("TRN2", target_bir_lowering=False, num_devices=1)
    arrays = {n: np.ascontiguousarray(inputs[n]) for n in _INS}
    arrays["ident"] = np.eye(128, dtype=np.float32)
    aps = {n: nc.dram_tensor(f"in_{n}", v.shape, mybir.dt.from_np(v.dtype), kind="ExternalInput").ap() for n, v in arrays.items()}
    out = nc.dram_tensor("out_0", (BATCH, CH, SIDE, SIDE), fp32, kind="ExternalOutput").ap()
    build(nc, aps, out)
    r = run_bass_kernel_spmd(nc, [{f"in_{n}": v for n, v in arrays.items()}], core_ids=[0])
    return r.results[0]["out_0"]
```
